# Optimizing a Trainium2 kernel written in Bass

```python
import numpy as np
import jax
import jax.numpy as jnp

def _softmax(x, axis=-1):
    return jax.nn.softmax(x, axis=axis)

def _gelu(x):
    return jax.nn.gelu(x, approximate=True)

def _silu(x):
    return jax.nn.silu(x)

def _sigmoid(x):
    return jax.nn.sigmoid(x)

def _layernorm(x, axis=-1, eps=1e-05):
    m = jnp.mean(x, axis=axis, keepdims=True)
    v = jnp.var(x, axis=axis, keepdims=True)
    return (x - m) / jnp.sqrt(v + eps)

def _scatter_add(tgt, idx, src, axis=0):
    return tgt.at[idx].add(src)

def _segment_sum(src, seg, n):
    return jax.ops.segment_sum(src, seg, n)
kernel_name = 'mk_xattn_ffn_d1_seqx_r4_cc687d'

def setup_inputs(seed: int=0):
    np.random.seed(seed)
    _w = jnp.asarray

    def _rec_inputs():
        import jax
        import jax.numpy as jnp
        _rk = jax.random.key(seed)
        x = -0.0002928 + 1 * jax.random.normal(jax.random.fold_in(_rk, 1), (2, 1024, 256), jnp.float32)
        _lenS = 1024 - jax.random.randint(jax.random.fold_in(_rk, 7), (2,), 0, max(1, 1024 // 4) + 1, jnp.int32)
        _lenS2 = 77 - jax.random.randint(jax.random.fold_in(_rk, 8), (2,), 0, max(1, 77 // 4) + 1, jnp.int32)
        _ctx_1024P = jax.random.normal(jax.random.fold_in(_rk, 11), (2, 16, 256), jnp.float32)
        _ctx_1024c = jax.random.dirichlet(jax.random.fold_in(_rk, 511), 0.3 * jnp.ones((16,), jnp.float32), (2, 77))
        _ctx_1024t = jnp.einsum('bsk,bkd->bsd', _ctx_1024c, _ctx_1024P)
        _ctx_1024t = _ctx_1024t * jax.lax.rsqrt(jnp.mean(jnp.square(_ctx_1024t)) + 1e-12) * 0.953939
        ctx_1024 = 2.81802e-05 + 1.00001 * (_ctx_1024t + 0.3 * jax.random.normal(jax.random.fold_in(_rk, 611), (2, 77, 256), jnp.float32))
        return (x, ctx_1024)
    x, ctx_1024 = _rec_inputs()

    def _L0_xattn_setup():
        import jax, jax.numpy as jnp
        import numpy as np
        D_MODEL = 256
        N_HEADS = 16
        HEAD_DIM = D_MODEL // N_HEADS
        key = jax.random.key(seed)
        k1, k2, k3, k4, k5, k6 = jax.random.split(key, 6)
        B, T_q, T_kv = (4, 256, 1024)
        s = 1.0 / np.sqrt(D_MODEL)
        return {'query': jax.random.normal(k1, (B, T_q, D_MODEL), dtype=jnp.float32), 'kv_source': jax.random.normal(k2, (B, T_kv, D_MODEL), dtype=jnp.float32), 'w_q': jax.random.normal(k3, (D_MODEL, D_MODEL), dtype=jnp.float32) * s, 'w_k': jax.random.normal(k4, (D_MODEL, D_MODEL), dtype=jnp.float32) * s, 'w_v': jax.random.normal(k5, (D_MODEL, D_MODEL), dtype=jnp.float32) * s, 'w_o': jax.random.normal(k6, (D_MODEL, D_MODEL), dtype=jnp.float32) * s}
    _L0_xattn_all = _L0_xattn_setup()
    _L0_xattn_in = {k: v for k, v in _L0_xattn_all.items() if k in ('w_q', 'w_k', 'w_v', 'w_o')}
    del _L0_xattn_all

    def _L0_ffn_setup():
        import jax, jax.numpy as jnp
        import numpy as np
        NUM_EXPERTS = 8
        TOP_K = 2
        ROUTE_SCALE = 1.0
        DIM = 256
        HID = 256
        B, S = (2, 1024)
        key = jax.random.key(seed)
        ks = jax.random.split(key, 9)
        sc = 0.05
        return {'x': jax.random.normal(ks[0], (B, S, DIM), dtype=jnp.float32), 'gate_w': jax.random.normal(ks[1], (NUM_EXPERTS, DIM), dtype=jnp.float32) * sc, 'w1': jax.random.normal(ks[2], (NUM_EXPERTS, HID, DIM), dtype=jnp.float32) * sc, 'w2': jax.random.normal(ks[3], (NUM_EXPERTS, DIM, HID), dtype=jnp.float32) * sc, 'w3': jax.random.normal(ks[4], (NUM_EXPERTS, HID, DIM), dtype=jnp.float32) * sc, 'sw1': jax.random.normal(ks[5], (HID, DIM), dtype=jnp.float32) * sc, 'sw2': jax.random.normal(ks[6], (DIM, HID), dtype=jnp.float32) * sc, 'sw3': jax.random.normal(ks[7], (HID, DIM), dtype=jnp.float32) * sc, 'expert_bias': jnp.zeros((NUM_EXPERTS,), dtype=jnp.float32)}
    _L0_ffn_all = _L0_ffn_setup()
    _L0_ffn_in = {k: v for k, v in _L0_ffn_all.items() if k in ('gate_w', 'w1', 'w2', 'w3', 'sw1', 'sw2', 'sw3', 'expert_bias')}
    del _L0_ffn_all
    return {'x': x, 'ctx_1024': ctx_1024, 'L0_xattn_w_q': _L0_xattn_in['w_q'], 'L0_xattn_w_k': _L0_xattn_in['w_k'], 'L0_xattn_w_v': _L0_xattn_in['w_v'], 'L0_xattn_w_o': _L0_xattn_in['w_o'], 'L0_ffn_gate_w': _L0_ffn_in['gate_w'], 'L0_ffn_w1': _L0_ffn_in['w1'], 'L0_ffn_w2': _L0_ffn_in['w2'], 'L0_ffn_w3': _L0_ffn_in['w3'], 'L0_ffn_sw1': _L0_ffn_in['sw1'], 'L0_ffn_sw2': _L0_ffn_in['sw2'], 'L0_ffn_sw3': _L0_ffn_in['sw3'], 'L0_ffn_expert_bias': _L0_ffn_in['expert_bias']}

def reference(x, ctx_1024, L0_xattn_w_q, L0_xattn_w_k, L0_xattn_w_v, L0_xattn_w_o, L0_ffn_gate_w, L0_ffn_w1, L0_ffn_w2, L0_ffn_w3, L0_ffn_sw1, L0_ffn_sw2, L0_ffn_sw3, L0_ffn_expert_bias):
    import jax
    import jax.numpy as jnp

    def _L0_xattn_ref(query, kv_source, w_q, w_k, w_v, w_o):
        import jax, jax.numpy as jnp
        import numpy as np
        D_MODEL = 256
        N_HEADS = 16
        HEAD_DIM = D_MODEL // N_HEADS
        B, T_q, _ = query.shape
        T_kv = kv_source.shape[1]
        q = (query @ w_q.T).reshape(B, T_q, N_HEADS, HEAD_DIM)
        k = (kv_source @ w_k.T).reshape(B, T_kv, N_HEADS, HEAD_DIM)
        v = (kv_source @ w_v.T).reshape(B, T_kv, N_HEADS, HEAD_DIM)
        scale = HEAD_DIM ** (-0.5)
        attn = jax.nn.softmax(jnp.einsum('bqhd,bkhd->bhqk', q, k) * scale, axis=-1)
        out = jnp.einsum('bhqk,bkhd->bqhd', attn, v).reshape(B, T_q, D_MODEL)
        return out @ w_o.T

    def _L0_ffn_ref(x, gate_w, w1, w2, w3, sw1, sw2, sw3, expert_bias):
        import jax, jax.numpy as jnp
        import numpy as np
        NUM_EXPERTS = 8
        TOP_K = 2
        ROUTE_SCALE = 1.0
        DIM = 256
        HID = 256
        B, S = (2, 1024)
        bs, slen, dim = x.shape
        xf = x.reshape(-1, dim)
        scores = jax.nn.sigmoid((xf @ gate_w.T).astype(jnp.float32))
        _, sel = jax.lax.top_k(scores + expert_bias[None, :], TOP_K)
        top_scores = jnp.take_along_axis(scores, sel, axis=1) * ROUTE_SCALE
        flat_sel = sel.reshape(-1)
        order = jnp.argsort(flat_sel, stable=True)
        scores_sorted = top_scores.reshape(-1)[order]
        tok_idx = order // TOP_K
        expert_ids = flat_sel[order]
        routed = xf[tok_idx]
        routed = (routed.astype(jnp.float32) * scores_sorted[:, None]).astype(x.dtype)
        out_r = jnp.zeros_like(routed)
        for e in range(NUM_EXPERTS):
            m = (expert_ids == e)[:, None]
            h = jax.nn.silu(routed @ w1[e].T) * (routed @ w3[e].T)
            out_r = out_r + jnp.where(m, h @ w2[e].T, jnp.zeros((), routed.dtype))
        shared = jax.nn.silu(xf @ sw1.T) * (xf @ sw3.T) @ sw2.T
        out_r = (out_r.astype(jnp.float32) * scores_sorted[:, None]).astype(x.dtype)
        out = shared.at[tok_idx].add(out_r)
        return out.reshape(bs, slen, dim)
    x = x + _L0_xattn_ref(_layernorm(x, axis=-1), ctx_1024, L0_xattn_w_q, L0_xattn_w_k, L0_xattn_w_v, L0_xattn_w_o)
    x = x + _L0_ffn_ref(_layernorm(x, axis=-1), L0_ffn_gate_w, L0_ffn_w1, L0_ffn_w2, L0_ffn_w3, L0_ffn_sw1, L0_ffn_sw2, L0_ffn_sw3, L0_ffn_expert_bias)
    return x

_drawn_inputs = setup_inputs


def setup_inputs(seed=0):
    import zlib

    import numpy as np

    out = dict(_drawn_inputs(seed))
    spreads = {'L0_ffn_expert_bias': (0.0, 0.1)}
    factors = {}
    for name, (base, spread) in spreads.items():
        noise = np.random.default_rng([zlib.crc32(name.encode()), seed]).standard_normal(out[name].shape)
        drawn = base * np.exp(spread * noise) if base else spread * noise
        out[name] = jnp.asarray(drawn.astype(out[name].dtype))
    for name, factor in factors.items():
        out[name] = (out[name] * factor).astype(out[name].dtype)
    return out
```

```python
import numpy as np
import concourse.bass as bass
from concourse import mybir

F32 = mybir.dt.float32
F32R = mybir.dt.float32r
BF16 = mybir.dt.bfloat16
I32 = mybir.dt.int32
U32 = mybir.dt.uint32
ALU = mybir.AluOpType
ACT = mybir.ActivationFunctionType
AXX = mybir.AxisListType.X

P = 128
BATCH, SEQ, DIM = 2, 1024, 256
KEYS, HEADS = 77, 16
HD = DIM // HEADS
TOKENS = BATCH * SEQ
TILES = TOKENS // P
TILES_PER_BATCH = SEQ // P
KT = DIM // P
EXPERTS, TOPK = 8, 2
EPS = 1e-5
BANK = 512
HEADS_PER_BANK = 4
BANK_COLS = HEADS_PER_BANK * KEYS
HALF_COLS = HEADS * KEYS // 2
CHUNKS = -(-HEADS * KEYS // P)
PCOLS = CHUNKS * P
VHEADS = 3
VN = CHUNKS * VHEADS
HV = HD + 1
UP = 2 * DIM
EW = KT * UP + KT * DIM
REGION = TOKENS + P
TILES_B = TOPK * TOKENS // P + EXPERTS - 1
SPLIT_STEPS = 12
SPLIT = EXPERTS * EW // SPLIT_STEPS
GATHER_BUFS = 4

FIRST, LAST = -2, TILES + 2
ROUTE_LINKS, ROUTE_SCORES, ROUTE_MASK, ROUTE_DEST = 13, 8, 10, 13
TABLE_COUNTS, TABLE_TILES = 2, 17


def head_base(c):
    return min(P * c // KEYS, HEADS - VHEADS)


def need(eng, semaphore, value):
    if not isinstance(value, int) or value > 0:
        eng.wait_ge(semaphore, value)


def live(known, shift):
    return known is None or 0 <= known + shift < TILES


def splitting(known):
    return known is None or 2 <= known < 2 + SPLIT_STEPS


def run_phase_a(eng, step):
    for i in range(FIRST, 4):
        step(i, i % 2, i, 0)
    for batch, (lo, hi) in enumerate(((4, TILES_PER_BATCH), (TILES_PER_BATCH, TILES - 2))):
        with eng.Fori(lo // 2, hi // 2) as turn:
            for par in range(2):
                step(turn * 2 + par, par, None, batch)
    for i in range(TILES - 2, LAST):
        step(i, i % 2, i, 1)


def run_phase_b(eng, step):
    for j in range(2):
        step(j, j, j)
    with eng.Fori(1, (TILES_B - 3) // 2) as turn:
        for par in range(2):
            step(turn * 2 + par, par, None)
    for j in range(TILES_B - 3, TILES_B):
        step(j, j % 2, j)


def cols(n, width=DIM):
    return bass.ds(n * width, width)


def v3(t, a):
    return t.rearrange("p (a b) -> p a b", a=a)


def layer_kernel(nc, x, ctxt, wqt, wkt, wvt, wot, gatet, bias, wffn, out):
    def sb(name, n, dt=F32):
        return nc.alloc_sbuf_tensor(name, [P, n], dt)

    lists = nc.dram_tensor("lists", [EXPERTS * REGION, DIM], F32, kind="Internal").ap()
    results = nc.dram_tensor("results", [TILES_B * P, DIM], F32, kind="Internal").ap()

    resid = sb("resid", TILES * DIM)
    wq, wk, wv, wo = (sb(n, KT * DIM) for n in ("wq", "wk", "wv", "wo"))
    gate_raw = sb("gate_raw", KT * EXPERTS)
    gate_hi = sb("gate_hi", KT * EXPERTS, F32R)
    gate_lo = sb("gate_lo", KT * EXPERTS, F32R)
    bias_b = sb("bias_b", EXPERTS)
    ctx_t = sb("ctx_t", KT * BATCH * 3 * KEYS)
    w_stage = sb("w_stage", 2 * SPLIT)
    w_hi = sb("w_hi", (EXPERTS + 1) * EW, F32R)
    w_lo = sb("w_lo", (EXPERTS + 1) * EW, F32R)
    k_raw = sb("k_raw", 2 * BATCH * KEYS)
    k_raw_hi = sb("k_raw_hi", 2 * BATCH * KEYS, F32R)
    k_raw_lo = sb("k_raw_lo", 2 * BATCH * KEYS, F32R)
    k_hi = sb("k_hi", BATCH * 2 * BANK_COLS, F32R)
    k_lo = sb("k_lo", BATCH * 2 * BANK_COLS, F32R)
    vals = sb("vals", BATCH * VN * HV)
    ident = sb("ident", P)
    head_of, head_mask = sb("head_of", 2 * HEADS_PER_BANK), sb("head_mask", HEADS_PER_BANK)
    val_mask = sb("val_mask", VN)
    upper = sb("upper", P, BF16)
    ones = sb("ones", P, BF16)
    minus_half = sb("minus_half", 1)
    iota_e = sb("iota_e", EXPERTS)
    iota_m = sb("iota_m", TILES)
    iota_j = sb("iota_j", TILES_B)
    ones_e = sb("ones_e", EXPERTS)
    zeros = sb("zeros", DIM)
    stats1, mv1, ve1, rstd1 = sb("stats1", 6), sb("mv1", 2), sb("ve1", 1), sb("rstd1", 1)
    stats2, mv2, ve2, rstd2 = sb("stats2", 6), sb("mv2", 2), sb("ve2", 1), sb("rstd2", 1)
    xn, xn_t = sb("xn", DIM), sb("xn_t", DIM)
    q_hi, q_lo = sb("q_hi", DIM, F32R), sb("q_lo", DIM, F32R)
    row_max, row_inv = sb("row_max", HEADS), sb("row_inv", HEADS)
    shared_space = sb("shared_space", 2 * PCOLS)
    probs, probs_t = shared_space[:, 0:PCOLS], shared_space[:, PCOLS:2 * PCOLS]
    gathered = shared_space[:, 0:GATHER_BUFS * TOPK * DIM]
    attn, attn_t = sb("attn", DIM), sb("attn_t", DIM)
    xn2 = sb("xn2", 2 * DIM)
    x2_hi, x2_lo = sb("x2_hi", 2 * DIM, F32R), sb("x2_lo", 2 * DIM, F32R)
    act_s, silu_s, hid = sb("act_s", DIM), sb("silu_s", DIM), sb("hid", DIM)
    h_hi, h_lo = sb("h_hi", DIM, F32R), sb("h_lo", DIM, F32R)
    th8, score, ranked, top8 = (sb(n, EXPERTS) for n in ("th8", "score", "ranked", "top8"))
    top8_i = sb("top8_i", EXPERTS, U32)
    chosen_f = sb("chosen_f", TOPK)
    picked = sb("picked", TOPK * EXPERTS)
    mask_bf, mask_sum = sb("mask_bf", EXPERTS, BF16), sb("mask_sum", EXPERTS, BF16)
    onehot = sb("onehot", TILES * TOPK * EXPERTS)
    scores2, ranks2 = sb("scores2", TILES * TOPK), sb("ranks2", TILES * TOPK)
    dest_f, dest = sb("dest_f", TOPK), sb("dest", 2 * TOPK, I32)
    scaled = sb("scaled", 2 * TOPK * DIM)
    counts, counts_i = sb("counts", EXPERTS), sb("counts_i", EXPERTS, I32)
    over = sb("over", EXPERTS * TILES)
    n_tiles, end_tile, start_tile = (sb(n, EXPERTS) for n in ("n_tiles", "end_tile", "start_tile"))
    last_tile, tile_j = sb("last_tile", 1), sb("tile_j", TILES_B)
    passed, passed_n = sb("passed", TILES_B * EXPERTS), sb("passed_n", TILES_B * EXPERTS)
    expert_f, before_f, row_f = (sb(n, TILES_B) for n in ("expert_f", "before_f", "row_f"))
    expert_i, row_i = sb("expert_i", TILES_B, I32), sb("row_i", TILES_B, I32)
    got_all = sb("got_all", TILES * TOPK * EXPERTS)
    got_f, got_i = sb("got_f", TILES * TOPK), sb("got_i", TILES * TOPK, I32)
    list_rows, y_rows = sb("list_rows", 2 * DIM), sb("y_rows", 2 * DIM)

    psum = nc.alloc_psum_tensor("psum", [P, 8 * BANK], F32)
    bank = [psum[:, n * BANK:(n + 1) * BANK] for n in range(8)]
    o_b, q_b, t_b, h_b = bank[4:8]
    score_view = (psum[:, 0:4 * BANK].rearrange("p (g c) -> p g c", g=4)[:, :, 0:BANK_COLS]
                  .rearrange("p g (h k) -> p g h k", k=KEYS))

    s = {name: nc.alloc_semaphore(name) for name in (
        "x0_in x_in ctx_in wk_in wq_in wv_in wo_in gate_in bias_in shared_in split_in0 split_in1 "
        "filled masked zeros_done k_ps k_out k_low k_masked v_ps v_done gate_high gate_low "
        "shared_hi shared_lo split_hi split_lo "
        "ln1_step pow1 xn1 t1_ps t1_out q_ps q_high q_low s_ps maxed subbed exped pt_ps pt_out "
        "pv_ps inv_done normed ot_ps ot_out o_ps x1_done ln2_step pow2 xn2_done "
        "t2_ps x2_high x2_low h_ps tanh_h silu_done hid_done gate_ps tanh_g route_step scaled_done "
        "rank_ps rank_read scat0 scat1 ht_ps h_high h_low y_ps acc_done count_ps table_step got_step pad_out "
        "b_in0 b_in1 b_t_ps b_x_high b_x_low b_h_ps b_silu b_hid b_ht_ps b_h_high b_h_low b_y_ps "
        "b_y b_out0 b_out1 c_in0 c_in1 c_in2 c_in3 c_first c_sum c_out").split()}
    split_in, scat = [s["split_in0"], s["split_in1"]], [s["scat0"], s["scat1"]]
    b_in, b_out = [s["b_in0"], s["b_in1"]], [s["b_out0"], s["b_out1"]]
    c_in = [s[f"c_in{n}"] for n in range(GATHER_BUFS)]

    with nc.Block() as block:

        @block.sync
        def _(sp):
            sp.dma_start(ctx_t[:, :], ctxt).then_inc(s["ctx_in"], 16)
            sp.dma_start(wk[:, :], wkt).then_inc(s["wk_in"], 16)
            x_tiles = x.rearrange("(t p) d -> p t d", p=P)
            resid_tiles = resid[:, :].rearrange("p (t d) -> p t d", d=DIM)
            sp.dma_start(resid_tiles[:, 0:2, :], x_tiles[:, 0:2, :]).then_inc(s["x0_in"], 16)
            sp.dma_start(wv[:, :], wvt).then_inc(s["wv_in"], 16)
            sp.dma_start(wo[:, :], wot).then_inc(s["wo_in"], 16)
            for a in (2, 9):
                sp.dma_start(resid_tiles[:, a:a + 7, :], x_tiles[:, a:a + 7, :]).then_inc(s["x_in"], 16)

            sp.dma_start(w_stage[:, 0:EW], wffn[:, EXPERTS * EW:(EXPERTS + 1) * EW]).then_inc(s["shared_in"], 16)
            sp.wait_ge(s["shared_lo"], 1)
            for n in range(2):
                sp.dma_start(w_stage[:, n * SPLIT:(n + 1) * SPLIT],
                             wffn[:, n * SPLIT:(n + 1) * SPLIT]).then_inc(split_in[n], 16)
            with sp.Fori(0, SPLIT_STEPS // 2 - 1) as turn:
                for par in range(2):
                    sp.wait_ge(s["split_lo"], turn * 2 + par + 1)
                    sp.dma_start(w_stage[:, cols(par, SPLIT)],
                                 wffn[:, cols(turn * 2 + par + 2, SPLIT)]).then_inc(split_in[par], 16)

            sp.wait_ge(s["table_step"], TABLE_COUNTS)
            sp.wait_ge(s["zeros_done"], 1)
            for e in range(EXPERTS):
                n_rows = sp.value_load(counts_i[0:1, e:e + 1], min_val=0, max_val=TOKENS)
                sp.dma_start(lists[bass.ds(n_rows + e * REGION, P), :], zeros[:, :]).then_inc(s["pad_out"], 16)
            sp.wait_ge(s["pad_out"], 16 * EXPERTS)
            for par in range(2):
                sp.wait_ge(scat[par], 16 * TOPK * (TILES // 2))
            sp.wait_ge(s["table_step"], TABLE_TILES)

            def load(j, par):
                row = sp.value_load(row_i[0:1, bass.ds(j, 1)], min_val=0, max_val=EXPERTS * REGION - P)
                sp.dma_start(list_rows[:, cols(par)], lists[bass.ds(row, P), :]).then_inc(b_in[par], 16)

            def store(j, par):
                sp.wait_ge(s["b_y"], j + 1)
                sp.dma_start(results[cols(j, P), :], y_rows[:, cols(par)]).then_inc(b_out[par], 16)

            for j in range(4):
                need(sp, s["b_t_ps"], j - 1)
                load(j, j % 2)
            with sp.Fori(0, (TILES_B - 5) // 2) as turn:
                for par in range(2):
                    sp.wait_ge(s["b_t_ps"], turn * 2 + par + 3)
                    load(turn * 2 + par + 4, par)
                    store(turn * 2 + par, par)
            for j in range(TILES_B - 5, TILES_B):
                if j + 4 < TILES_B:
                    sp.wait_ge(s["b_t_ps"], j + 3)
                    load(j + 4, j % 2)
                store(j, j % 2)

            with sp.Fori(0, TILES) as t:
                sp.wait_ge(s["c_sum"], t + 1)
                sp.dma_start(out[cols(t, P), :], resid[:, cols(t)]).then_inc(s["c_out"], 16)
            sp.wait_ge(s["c_out"], 16 * TILES)

        @block.gpsimd
        def _(pool):
            fills = ((ident, 0.0), (head_of, 1.0), (val_mask, 1.0), (upper, 1.0), (ones, 1.0),
                     (minus_half, -0.5), (mask_sum, 0.0), (mask_bf, 0.0), (ones_e, 1.0))
            for t, value in fills:
                pool.memset(t[:, :], value).then_inc(s["filled"], 1)
            pool.memset(probs[:, HEADS * KEYS:PCOLS], 0.0).then_inc(s["filled"], 1)
            for t, pitch, n in ((iota_e, 1, EXPERTS), (iota_m, P, TILES), (iota_j, 1, TILES_B)):
                pool.iota(t[:, :], pattern=[[pitch, n]], base=0, channel_multiplier=0,
                          allow_small_or_imprecise_dtypes=True).then_inc(s["filled"], 1)
            pool.wait_ge(s["filled"], 13)

            def cut(t, op, fill, base, pattern, per_partition):
                pool.affine_select(out=t, in_=t, compare_op=op, fill=fill, base=base, pattern=[pattern],
                                   channel_multiplier=per_partition).then_inc(s["masked"], 1)

            cut(ident[:, :], ALU.not_equal, 1.0, 0, [-1, P], 1)
            cut(head_of[:, :], ALU.is_ge, 0.0, 0, [-HD, 2 * HEADS_PER_BANK], 1)
            pool.wait_ge(s["masked"], 2)
            cut(head_of[:, :], ALU.is_ge, 0.0, HD - 1, [HD, 2 * HEADS_PER_BANK], -1)
            pool.wait_ge(s["masked"], 3)
            pool.tensor_tensor(head_mask[:, :], head_of[:, 0:HEADS_PER_BANK], head_of[:, HEADS_PER_BANK:],
                               ALU.add).then_inc(s["masked"], 1)
            for c in range(CHUNKS):
                cut(val_mask[:, cols(c, VHEADS)], ALU.is_ge, 0.0, P * c - KEYS * head_base(c),
                    [-KEYS, VHEADS], 1)
            pool.wait_ge(s["masked"], 4 + CHUNKS)
            for c in range(CHUNKS):
                cut(val_mask[:, cols(c, VHEADS)], ALU.is_ge, 0.0, KEYS * head_base(c) + KEYS - 1 - P * c,
                    [KEYS, VHEADS], -1)
            cut(upper[:, :], ALU.is_ge, 0.0, -1, [1, P], -1)
            pool.memset(zeros[:, :], 0.0).then_inc(s["zeros_done"], 1)

            def scatter(par):
                for k in range(TOPK):
                    n = par * TOPK + k
                    pool.indirect_dma_start(
                        lists, bass.IndirectOffsetOnAxis(ap=dest[:, n:n + 1], axis=0),
                        scaled[:, cols(n)], None).then_inc(scat[par], 16)

            def step(i, par, known, _):
                if live(known, -3):
                    pool.wait_ge(s["scaled_done"], TOPK * (i - 2))
                    need(pool, s["route_step"], (i - 2) * ROUTE_LINKS)
                if live(known, -1):
                    pool.wait_ge(s["ln2_step"], 3 * i)
                    pool.tensor_tensor(rstd2[:, :], ve2[:, :], minus_half[:, :], ALU.pow).then_inc(s["pow2"], 1)
                if live(known, -3):
                    scatter(1 - par)
                if live(known, 2):
                    pool.wait_ge(s["ln1_step"], 3 * (i + 3))
                    pool.tensor_tensor(rstd1[:, :], ve1[:, :], minus_half[:, :], ALU.pow).then_inc(s["pow1"], 1)
                if known == -1:
                    pool.wait_ge(s["shared_hi"], 1)
                    pool.tensor_tensor(w_lo[:, cols(EXPERTS, EW)], w_stage[:, 0:EW],
                                       w_hi[:, cols(EXPERTS, EW)].bitcast(F32),
                                       ALU.subtract).then_inc(s["shared_lo"], 1)
                if splitting(known):
                    pool.wait_ge(s["split_hi"], i - 1)
                    pool.tensor_tensor(w_lo[:, cols(i - 2, SPLIT)], w_stage[:, cols(par, SPLIT)],
                                       w_hi[:, cols(i - 2, SPLIT)].bitcast(F32),
                                       ALU.subtract).then_inc(s["split_lo"], 1)
                if live(known, -2):
                    pool.wait_ge(s["route_step"], (i - 2) * ROUTE_LINKS + ROUTE_SCORES)
                    need(pool, scat[par], (i - 2 - par) * 8 * TOPK)
                    for k in range(TOPK):
                        score_k = scores2[:, cols((i - 2) * TOPK + k, 1)]
                        pool.tensor_tensor(scaled[:, cols(par * TOPK + k)], xn2[:, cols(par)],
                                           score_k.to_broadcast([P, DIM]), ALU.mult).then_inc(s["scaled_done"], 1)

            run_phase_a(pool, step)
            pool.wait_ge(s["scaled_done"], TOPK * TILES)
            pool.wait_ge(s["route_step"], ROUTE_LINKS * TILES)
            scatter((TILES - 1) % 2)

            pool.wait_ge(s["got_step"], 5)
            for par in range(2):
                pool.wait_ge(b_out[par], 16 * ((TILES_B + 1 - par) // 2))
            for t in range(TILES):
                n = t % GATHER_BUFS
                need(pool, s["c_sum"], t - GATHER_BUFS + 1)
                for k in range(TOPK):
                    pool.indirect_dma_start(
                        gathered[:, cols(n * TOPK + k)], None, results,
                        bass.IndirectOffsetOnAxis(ap=got_i[:, t * TOPK + k:t * TOPK + k + 1], axis=0),
                    ).then_inc(c_in[n], 16)

        @block.scalar
        def _(act):
            act.dma_start(wq[:, :], wqt).then_inc(s["wq_in"], 16)
            act.dma_start(gate_raw[:, :], gatet).then_inc(s["gate_in"], 16)
            act.dma_start(bias_b[:, :], bias.partition_broadcast(P)).then_inc(s["bias_in"], 16)
            act.wait_ge(s["k_ps"], 1)
            act.activation(k_raw[:, :], h_b[:, 0:2 * BATCH * KEYS], ACT.Copy).then_inc(s["k_out"], 1)
            act.wait_ge(s["k_out"], 1)
            act.activation(k_raw_hi[:, :], k_raw[:, :], ACT.Copy).then_inc(s["k_out"], 1)
            act.wait_ge(s["gate_in"], 16)
            act.activation(gate_hi[:, :], gate_raw[:, :], ACT.Copy).then_inc(s["gate_high"], 1)

            def step(i, par, known, _):
                if live(known, 1):
                    act.wait_ge(s["t1_ps"], i + 2)
                    act.activation(xn_t[:, :], q_b[:, 0:DIM], ACT.Copy).then_inc(s["t1_out"], 1)
                if live(known, -2):
                    act.wait_ge(s["t2_ps"], i - 1)
                    act.activation(x2_hi[:, 0:DIM], t_b[:, 0:DIM], ACT.Copy).then_inc(s["x2_high"], 1)
                if live(known, 1):
                    act.wait_ge(s["q_ps"], i + 2)
                    act.activation(q_hi[:, :], q_b[:, 0:DIM], ACT.Copy).then_inc(s["q_high"], 1)
                if live(known, 0):
                    for g in range(2):
                        act.wait_ge(s["subbed"], 2 * i + g + 1)
                        part = probs[:, cols(g, HALF_COLS)]
                        act.activation(part, part, ACT.Exp, scale=float(HD) ** -0.5).then_inc(s["exped"], 1)
                if live(known, -2):
                    act.wait_ge(s["h_ps"], i - 1)
                    need(act, s["silu_done"], i - 2)
                    act.activation(act_s[:, :], h_b[:, 0:DIM], ACT.Tanh, scale=0.5).then_inc(s["tanh_h"], 1)
                    act.wait_ge(s["gate_ps"], i - 1)
                    act.activation(th8[:, :], t_b[:, 0:EXPERTS], ACT.Tanh, scale=0.5).then_inc(s["tanh_g"], 1)
                if live(known, 0):
                    for g in range(3):
                        act.wait_ge(s["pt_ps"], 3 * i + g + 1)
                        n = min(BANK, PCOLS - BANK * g)
                        act.activation(probs_t[:, BANK * g:BANK * g + n], bank[g][:, 0:n],
                                       ACT.Copy).then_inc(s["pt_out"], 1)
                if live(known, -2):
                    act.wait_ge(s["ht_ps"], i - 1)
                    act.activation(h_hi[:, :], t_b[:, 0:DIM], ACT.Copy).then_inc(s["h_high"], 1)
                if splitting(known):
                    act.wait_ge(split_in[par], (i - par) * 8)
                    act.activation(w_hi[:, cols(i - 2, SPLIT)], w_stage[:, cols(par, SPLIT)],
                                   ACT.Copy).then_inc(s["split_hi"], 1)
                if known == -1:
                    act.wait_ge(s["shared_in"], 16)
                    act.activation(w_hi[:, cols(EXPERTS, EW)], w_stage[:, 0:EW], ACT.Copy).then_inc(s["shared_hi"], 1)
                if live(known, 0):
                    act.wait_ge(s["ot_ps"], i + 1)
                    act.activation(attn_t[:, :], q_b[:, 0:DIM], ACT.Copy).then_inc(s["ot_out"], 1)

            run_phase_a(act, step)

            def x_high(j, par):
                act.wait_ge(s["b_t_ps"], j + 1)
                act.activation(x2_hi[:, cols(par)], q_b[:, 0:DIM], ACT.Copy).then_inc(s["b_x_high"], 1)

            def silu(j):
                act.wait_ge(s["b_h_ps"], j + 1)
                need(act, s["b_hid"], j)
                act.activation(act_s[:, :], h_b[:, 0:DIM], ACT.Silu).then_inc(s["b_silu"], 1)

            def step_b(j, par, known):
                if known is None or known + 2 < TILES_B:
                    x_high(j + 2, par)
                act.wait_ge(s["b_ht_ps"], j + 1)
                act.activation(h_hi[:, :], t_b[:, 0:DIM], ACT.Copy).then_inc(s["b_h_high"], 1)
                if known is None or known + 1 < TILES_B:
                    silu(j + 1)
                act.wait_ge(s["b_y_ps"], j + 1)
                need(act, b_out[par], (j - par) * 8)
                act.activation(y_rows[:, cols(par)], o_b[:, 0:DIM], ACT.Copy).then_inc(s["b_y"], 1)

            x_high(0, 0)
            x_high(1, 1)
            silu(0)
            run_phase_b(act, step_b)

        @block.vector
        def _(dve):
            tt, stt, ts = dve.tensor_tensor, dve.scalar_tensor_tensor, dve.tensor_scalar

            def chain(semaphore, before):
                count = [0]

                def link(ins, until=True):
                    count[0] += 1
                    ins.then_inc(semaphore, 1)
                    if until:
                        dve.wait_ge(semaphore, before + count[0])
                return link

            def values(b, source):
                dve.wait_ge(s["v_ps"], b + 1)
                view = v3(vals[:, cols(b, VN * HV)], VN)
                tt(view[:, :, 0:HD], v3(source[:, 0:VN * HD], VN),
                   val_mask[:, :].unsqueeze(2).to_broadcast([P, VN, HD]), ALU.mult).then_inc(s["v_done"], 1)
                dve.tensor_copy(view[:, :, HD:HV], val_mask[:, :].unsqueeze(2)).then_inc(s["v_done"], 1)

            dve.wait_ge(s["k_out"], 2)
            tt(k_raw_lo[:, :], k_raw[:, :], k_raw_hi[:, :].bitcast(F32), ALU.subtract).then_inc(s["k_low"], 1)
            dve.wait_ge(s["masked"], 4)
            dve.wait_ge(s["k_low"], 1)

            def keys(b):
                for half in range(2):
                    for raw, part in ((k_raw_hi, k_hi), (k_raw_lo, k_lo)):
                        tt(v3(part[:, cols(b * 2 + half, BANK_COLS)], HEADS_PER_BANK),
                           raw[:, cols(half * BATCH + b, KEYS)].bitcast(F32).unsqueeze(1)
                           .to_broadcast([P, HEADS_PER_BANK, KEYS]),
                           head_mask[:, :].unsqueeze(2).to_broadcast([P, HEADS_PER_BANK, KEYS]),
                           ALU.mult).then_inc(s["k_masked"], 1)

            def step(i, par, known, _):
                if live(known, 0):
                    dve.wait_ge(s["s_ps"], i + 1)
                    dve.tensor_reduce(v3(row_max[:, :], 4), score_view, axis=AXX, op=ALU.max).then_inc(s["maxed"], 1)
                if live(known, -1):
                    dve.wait_ge(s["o_ps"], i)
                    x1 = resid[:, cols(i - 1)]
                    tt(x1, x1, o_b[:, 0:DIM], ALU.add).then_inc(s["x1_done"], 1)
                if live(known, -2):
                    dve.wait_ge(s["x2_high"], i - 1)
                    tt(x2_lo[:, 0:DIM], t_b[:, 0:DIM], x2_hi[:, 0:DIM].bitcast(F32),
                       ALU.subtract).then_inc(s["x2_low"], 1)
                if live(known, 0):
                    dve.wait_ge(s["maxed"], i + 1)
                    for g in range(2):
                        tt(probs[:, cols(g, HALF_COLS)].rearrange("p (b h k) -> p b h k", b=2, k=KEYS),
                           score_view[:, 2 * g:2 * g + 2, :, :],
                           v3(row_max[:, cols(g, HEADS // 2)], 2).unsqueeze(3)
                           .to_broadcast([P, 2, HEADS_PER_BANK, KEYS]), ALU.subtract).then_inc(s["subbed"], 1)
                if live(known, -1):
                    dve.wait_ge(s["x1_done"], i)
                if live(known, 1):
                    dve.wait_ge(s["q_high"], i + 2)
                    tt(q_lo[:, :], q_b[:, 0:DIM], q_hi[:, :].bitcast(F32), ALU.subtract).then_inc(s["q_low"], 1)
                norms = []
                if live(known, -1):
                    norms.append((s["ln2_step"], (i - 1) * 3, stats2, mv2, ve2, x1))
                if live(known, 2):
                    if known == FIRST:
                        dve.wait_ge(s["x0_in"], 16)
                    if known == 0:
                        dve.wait_ge(s["x_in"], 32)
                    x0 = resid[:, cols(i + 2)]
                    norms.append((s["ln1_step"], (i + 2) * 3, stats1, mv1, ve1, x0))
                for done, before, st, mv, ve, rows in norms:
                    dve.bn_stats(st[:, :], rows).then_inc(done, 1)
                for done, before, st, mv, ve, rows in norms:
                    dve.wait_ge(done, before + 1)
                if live(known, -2):
                    dve.wait_ge(s["tanh_h"], i - 1)
                    stt(silu_s[:, :], act_s[:, :], 1.0, h_b[:, 0:DIM], ALU.add, ALU.mult).then_inc(s["silu_done"], 1)
                for done, before, st, mv, ve, rows in norms:
                    dve.bn_aggr(mv[:, :], st[:, :]).then_inc(done, 1)
                if live(known, -2):
                    dve.wait_ge(s["silu_done"], i - 1)
                    stt(hid[:, :], silu_s[:, :], 0.5, h_b[:, DIM:2 * DIM], ALU.mult, ALU.mult).then_inc(s["hid_done"], 1)
                for done, before, st, mv, ve, rows in norms:
                    dve.wait_ge(done, before + 2)
                    ts(ve[:, :], mv[:, 1:2], EPS, None, ALU.add).then_inc(done, 1)
                if live(known, -2):
                    link = chain(s["route_step"], (i - 2) * ROUTE_LINKS)
                    hot = onehot[:, cols(i - 2, TOPK * EXPERTS)]
                    hot0 = onehot[:, cols((i - 2) * TOPK, EXPERTS)]
                    hot1 = onehot[:, cols((i - 2) * TOPK + 1, EXPERTS)]
                    dve.wait_ge(s["tanh_g"], i - 1)
                    link(ts(score[:, :], th8[:, :], 0.5, 0.5, ALU.mult, ALU.add))
                    link(tt(ranked[:, :], score[:, :], bias_b[:, :], ALU.add))
                if live(known, -1):
                    dve.wait_ge(s["pow2"], i)
                    need(dve, s["scaled_done"], TOPK * (i - 2))
                    ts(xn2[:, cols(1 - par)], x1, mv2[:, 0:1], rstd2[:, :],
                       ALU.subtract, ALU.mult).then_inc(s["xn2_done"], 1)
                if live(known, -2):
                    link(dve.max(top8[:, :], ranked[:, :]))
                if live(known, 2):
                    dve.wait_ge(s["pow1"], i + 3)
                    need(dve, s["t1_ps"], i + 2)
                    ts(xn[:, :], x0, mv1[:, 0:1], rstd1[:, :], ALU.subtract, ALU.mult).then_inc(s["xn1"], 1)
                if live(known, -2):
                    link(dve.max_index(top8_i[:, :], top8[:, :], ranked[:, :]))
                    link(dve.tensor_copy(chosen_f[:, :], top8_i[:, 0:TOPK]))
                    link(tt(v3(hot, TOPK), iota_e[:, :].unsqueeze(1).to_broadcast([P, TOPK, EXPERTS]),
                            chosen_f[:, :].unsqueeze(2).to_broadcast([P, TOPK, EXPERTS]), ALU.is_equal))
                    link(tt(v3(picked[:, :], TOPK), v3(hot, TOPK),
                            score[:, :].unsqueeze(1).to_broadcast([P, TOPK, EXPERTS]), ALU.mult))
                    link(dve.tensor_reduce(scores2[:, cols(i - 2, TOPK)], v3(picked[:, :], TOPK),
                                           axis=AXX, op=ALU.add))
                    need(dve, s["rank_ps"], i - 2)
                    link(tt(mask_sum[:, :], mask_sum[:, :], mask_bf[:, :], ALU.add))
                    link(tt(mask_bf[:, :], hot0, hot1, ALU.add))
                if live(known, -2):
                    dve.wait_ge(s["h_high"], i - 1)
                    tt(h_lo[:, :], t_b[:, 0:DIM], h_hi[:, :].bitcast(F32), ALU.subtract).then_inc(s["h_low"], 1)
                if live(known, 0):
                    dve.wait_ge(s["pv_ps"], i + 1)
                    o_heads = v3(o_b[:, 0:HEADS * HV], HEADS)
                    dve.reciprocal(row_inv[:, :].unsqueeze(2), o_heads[:, :, HD:HV]).then_inc(s["inv_done"], 1)
                    dve.wait_ge(s["inv_done"], i + 1)
                    tt(v3(attn[:, :], HEADS), o_heads[:, :, 0:HD],
                       row_inv[:, :].unsqueeze(2).to_broadcast([P, HEADS, HD]), ALU.mult).then_inc(s["normed"], 1)
                if live(known, -2):
                    dve.wait_ge(s["y_ps"], i - 1)
                    x2 = resid[:, cols(i - 2)]
                    tt(x2, x2, h_b[:, 0:DIM], ALU.add).then_inc(s["acc_done"], 1)
                    ranks = ranks2[:, cols(i - 2, TOPK)]
                    dve.wait_ge(s["rank_ps"], i - 1)
                    tt(v3(picked[:, :], TOPK), v3(hot, TOPK),
                       t_b[:, 0:EXPERTS].unsqueeze(1).to_broadcast([P, TOPK, EXPERTS]),
                       ALU.mult).then_inc(s["rank_read"], 1)
                    dve.wait_ge(s["rank_read"], i - 1)
                    link(dve.tensor_reduce(ranks, v3(picked[:, :], TOPK), axis=AXX, op=ALU.add))
                    link(stt(dest_f[:, :], chosen_f[:, :], float(REGION), ranks, ALU.mult, ALU.add))
                    need(dve, scat[par], (i - 2 - par) * 8 * TOPK)
                    link(dve.tensor_copy(dest[:, cols(par, TOPK)], dest_f[:, :]), until=False)
                if known == FIRST:
                    keys(0)
                    dve.wait_ge(s["masked"], 5 + 2 * CHUNKS)
                    values(0, t_b)
                    dve.wait_ge(s["gate_high"], 1)
                    tt(gate_lo[:, :], gate_raw[:, :], gate_hi[:, :].bitcast(F32), ALU.subtract).then_inc(s["gate_low"], 1)
                    dve.wait_ge(s["bias_in"], 16)
                    dve.wait_ge(s["filled"], 13)
                if known == 0:
                    keys(1)
                    values(1, h_b)

            run_phase_a(dve, step)

            link = chain(s["table_step"], 0)
            dve.wait_ge(s["count_ps"], 1)
            link(dve.tensor_copy(counts[:, :], t_b[:, 0:EXPERTS]))
            link(dve.tensor_copy(counts_i[:, :], counts[:, :]))
            link(tt(v3(over[:, :], EXPERTS), counts[:, :].unsqueeze(2).to_broadcast([P, EXPERTS, TILES]),
                    iota_m[:, :].unsqueeze(1).to_broadcast([P, EXPERTS, TILES]), ALU.is_gt))
            link(dve.tensor_reduce(n_tiles[:, :], v3(over[:, :], EXPERTS), axis=AXX, op=ALU.add))
            link(dve.tensor_tensor_scan(end_tile[:, :], ones_e[:, :], n_tiles[:, :], 0.0, ALU.mult, ALU.add))
            link(tt(start_tile[:, :], end_tile[:, :], n_tiles[:, :], ALU.subtract))
            link(ts(last_tile[:, :], end_tile[:, EXPERTS - 1:EXPERTS], -1.0, None, ALU.add))
            link(ts(tile_j[:, :], iota_j[:, :], last_tile[:, :], None, ALU.min))
            link(tt(v3(passed[:, :], TILES_B), tile_j[:, :].unsqueeze(2).to_broadcast([P, TILES_B, EXPERTS]),
                    end_tile[:, :].unsqueeze(1).to_broadcast([P, TILES_B, EXPERTS]), ALU.is_ge))
            link(dve.tensor_reduce(expert_f[:, :], v3(passed[:, :], TILES_B), axis=AXX, op=ALU.add))
            link(tt(v3(passed_n[:, :], TILES_B), v3(passed[:, :], TILES_B),
                    n_tiles[:, :].unsqueeze(1).to_broadcast([P, TILES_B, EXPERTS]), ALU.mult))
            link(dve.tensor_reduce(before_f[:, :], v3(passed_n[:, :], TILES_B), axis=AXX, op=ALU.add))
            link(dve.tensor_copy(expert_i[:, :], expert_f[:, :]))
            link(tt(row_f[:, :], tile_j[:, :], before_f[:, :], ALU.subtract))
            link(ts(before_f[:, :], expert_f[:, :], float(REGION), None, ALU.mult))
            link(stt(row_f[:, :], row_f[:, :], float(P), before_f[:, :], ALU.mult, ALU.add))
            link(dve.tensor_copy(row_i[:, :], row_f[:, :]))

            def x_low(j, par):
                dve.wait_ge(s["b_x_high"], j + 1)
                tt(x2_lo[:, cols(par)], q_b[:, 0:DIM], x2_hi[:, cols(par)].bitcast(F32),
                   ALU.subtract).then_inc(s["b_x_low"], 1)

            def hidden(j):
                dve.wait_ge(s["b_silu"], j + 1)
                tt(hid[:, :], act_s[:, :], h_b[:, DIM:2 * DIM], ALU.mult).then_inc(s["b_hid"], 1)

            def step_b(j, par, known):
                if known is None or known + 2 < TILES_B:
                    x_low(j + 2, par)
                dve.wait_ge(s["b_h_high"], j + 1)
                tt(h_lo[:, :], t_b[:, 0:DIM], h_hi[:, :].bitcast(F32), ALU.subtract).then_inc(s["b_h_low"], 1)
                if known is None or known + 1 < TILES_B:
                    hidden(j + 1)

            x_low(0, 0)
            x_low(1, 1)
            hidden(0)

            link = chain(s["got_step"], 0)
            choices = onehot[:, :].rearrange("p (a e) -> p a e", e=EXPERTS)
            link(tt(v3(got_all[:, :], TILES * TOPK), choices,
                    start_tile[:, :].unsqueeze(1).to_broadcast([P, TILES * TOPK, EXPERTS]), ALU.mult))
            link(dve.tensor_reduce(got_f[:, :], v3(got_all[:, :], TILES * TOPK), axis=AXX, op=ALU.add))
            link(stt(got_f[:, :], got_f[:, :], float(P), ranks2[:, :], ALU.mult, ALU.add))
            link(dve.tensor_copy(got_i[:, :], got_f[:, :]))
            link(dve.tensor_copy(top8[:, :], counts[:, :]))
            run_phase_b(dve, step_b)

            with dve.Fori(0, TILES // GATHER_BUFS) as turn:
                for n in range(GATHER_BUFS):
                    t = turn * GATHER_BUFS + n
                    acc = resid[:, cols(t)]
                    dve.wait_ge(c_in[n], turn * (16 * TOPK) + 16 * TOPK)
                    stt(acc, gathered[:, cols(n * TOPK)], scores2[:, cols(t * TOPK, 1)], acc,
                        ALU.mult, ALU.add).then_inc(s["c_first"], 1)
                    dve.wait_ge(s["c_first"], t + 1)
                    stt(acc, gathered[:, cols(n * TOPK + 1)], scores2[:, cols(t * TOPK + 1, 1)], acc,
                        ALU.mult, ALU.add).then_inc(s["c_sum"], 1)

        @block.tensor
        def _(pe):
            mm = pe.matmul

            def product(to, stationary, moving, start=True, stop=True):
                (ah, al), (bh, bl) = stationary, moving
                mm(to, ah, bl, start=start, stop=False)
                mm(to, al, bh, start=False, stop=False)
                return mm(to, ah, bh, start=False, stop=stop)

            def transposed(to, rows):
                for kt in range(KT):
                    last = pe.transpose(to[:, cols(kt, P)], rows[:, cols(kt, P)], ident[:, :])
                return last

            pe.wait_ge(s["ctx_in"], 16)
            pe.wait_ge(s["wk_in"], 16)
            for half in range(2):
                for kt in range(KT):
                    first_keys = (ctx_t[:, cols(kt, BATCH * 3 * KEYS)]
                                  .rearrange("p (b r) -> p b r", b=BATCH)[:, :, 0:KEYS])
                    last = mm(v3(h_b[:, cols(half, BATCH * KEYS)], BATCH),
                              wk[:, kt * DIM + half * P:kt * DIM + (half + 1) * P], first_keys,
                              start=kt == 0, stop=kt == KT - 1)
            last.then_inc(s["k_ps"], 1)

            def values(b, to):
                for c in range(CHUNKS):
                    for kt in range(KT):
                        a = (kt * BATCH + b) * 3 * KEYS + P * c % KEYS
                        w = kt * DIM + head_base(c) * HD
                        last = mm(to[:, cols(c, VHEADS * HD)], ctx_t[:, a:a + P],
                                  wv[:, w:w + VHEADS * HD], start=kt == 0, stop=kt == KT - 1)
                last.then_inc(s["v_ps"], 1)

            def step(i, par, known, batch):
                if live(known, 0):
                    if known == 0:
                        pe.wait_ge(s["k_masked"], 4)
                    if known is None and batch == 1:
                        pe.wait_ge(s["k_masked"], 8)
                    pe.wait_ge(s["q_low"], i + 1)
                    need(pe, s["pt_out"], 3 * i)
                    for half in range(2):
                        for r in range(2):
                            rows = slice(64 * r, 64 * r + 64)
                            q = [t[rows, cols(half, P)] for t in (q_hi, q_lo)]
                            k = [t[rows, cols(batch * 2 + half, BANK_COLS)] for t in (k_hi, k_lo)]
                            last = product(bank[2 * half + r][:, 0:BANK_COLS], q, k)
                    last.then_inc(s["s_ps"], 1)
                if live(known, 1):
                    if known == -1:
                        pe.wait_ge(s["masked"], 1)
                    pe.wait_ge(s["xn1"], i + 2)
                    need(pe, s["ot_out"], i)
                    transposed(q_b, xn).then_inc(s["t1_ps"], 1)
                if live(known, -1):
                    if known == 1:
                        pe.wait_ge(s["wo_in"], 16)
                    pe.wait_ge(s["ot_out"], i)
                    for kt in range(KT):
                        last = mm(o_b[:, 0:DIM], attn_t[:, cols(kt, P)], wo[:, cols(kt)],
                                  start=kt == 0, stop=kt == KT - 1)
                    last.then_inc(s["o_ps"], 1)
                if live(known, -2):
                    pe.wait_ge(s["xn2_done"], i - 1)
                    need(pe, s["rank_read"], i - 2)
                    transposed(t_b, xn2[:, cols(par)]).then_inc(s["t2_ps"], 1)
                if live(known, 1):
                    if known == -1:
                        pe.wait_ge(s["wq_in"], 16)
                    pe.wait_ge(s["t1_out"], i + 2)
                    for half in range(2):
                        for kt in range(KT):
                            last = mm(q_b[:, cols(half, P)], wq[:, kt * DIM + half * P:kt * DIM + (half + 1) * P],
                                      xn_t[:, cols(kt, P)], start=kt == 0, stop=kt == KT - 1)
                    last.then_inc(s["q_ps"], 1)
                if live(known, -2):
                    if known == 2:
                        pe.wait_ge(s["shared_lo"], 1)
                        pe.wait_ge(s["gate_low"], 1)
                    pe.wait_ge(s["x2_low"], i - 1)
                    need(pe, s["acc_done"], i - 2)
                    for kt in range(KT):
                        w = EXPERTS * EW + kt * UP
                        last = product(h_b, [t[:, cols(kt, P)] for t in (x2_hi, x2_lo)],
                                       [t[:, w:w + UP] for t in (w_hi, w_lo)],
                                       start=kt == 0, stop=kt == KT - 1)
                    last.then_inc(s["h_ps"], 1)
                    for kt in range(KT):
                        last = product(t_b[:, 0:EXPERTS], [t[:, cols(kt, P)] for t in (x2_hi, x2_lo)],
                                       [t[:, cols(kt, EXPERTS)] for t in (gate_hi, gate_lo)],
                                       start=kt == 0, stop=kt == KT - 1)
                    last.then_inc(s["gate_ps"], 1)
                if live(known, 0):
                    if known == 0:
                        pe.wait_ge(s["filled"], 13)
                    for c in range(CHUNKS):
                        if c in (0, 4):
                            pe.wait_ge(s["exped"], 2 * i + 1 + c // 4)
                        last = pe.transpose(bank[c // 4][:, cols(c % 4, P)], probs[:, cols(c, P)], ident[:, :])
                        if c % 4 == 3 or c == CHUNKS - 1:
                            last.then_inc(s["pt_ps"], 1)
                if live(known, -2):
                    pe.wait_ge(s["hid_done"], i - 1)
                    pe.wait_ge(s["tanh_g"], i - 1)
                    transposed(t_b, hid).then_inc(s["ht_ps"], 1)
                if live(known, 0):
                    if known == 0:
                        pe.wait_ge(s["v_done"], 2)
                    if known is None and batch == 1:
                        pe.wait_ge(s["v_done"], 4)
                    need(pe, s["x1_done"], i)
                    for c in range(CHUNKS):
                        if c % 4 == 0:
                            pe.wait_ge(s["pt_out"], 3 * i + c // 4 + 1)
                        last = mm(o_b[:, head_base(c) * HV:(head_base(c) + VHEADS) * HV],
                                  probs_t[:, cols(c, P)], vals[:, cols(batch * CHUNKS + c, VHEADS * HV)],
                                  start=c == 0, stop=c == CHUNKS - 1, skip_group_check=True)
                    last.then_inc(s["pv_ps"], 1)
                if live(known, -2):
                    pe.wait_ge(s["h_low"], i - 1)
                    for kt in range(KT):
                        w = EXPERTS * EW + KT * UP + kt * DIM
                        last = product(h_b[:, 0:DIM], [t[:, cols(kt, P)] for t in (h_hi, h_lo)],
                                       [t[:, w:w + DIM] for t in (w_hi, w_lo)],
                                       start=kt == 0, stop=kt == KT - 1)
                    last.then_inc(s["y_ps"], 1)
                    pe.wait_ge(s["route_step"], (i - 2) * ROUTE_LINKS + ROUTE_MASK)
                    mm(t_b[:, 0:EXPERTS], upper[:, :], mask_bf[:, :], start=True, stop=False)
                    mm(t_b[:, 0:EXPERTS], ones[:, :], mask_sum[:, :], start=False, stop=True).then_inc(s["rank_ps"], 1)
                if live(known, 0):
                    pe.wait_ge(s["normed"], i + 1)
                    pe.wait_ge(s["q_low"], min(i + 2, TILES) if known is not None else i + 2)
                    transposed(q_b, attn).then_inc(s["ot_ps"], 1)
                if known == FIRST:
                    pe.wait_ge(s["wv_in"], 16)
                    values(0, t_b)
                if known == 0:
                    pe.wait_ge(s["k_out"], 1)
                    values(1, h_b)

            run_phase_a(pe, step)

            pe.wait_ge(s["rank_read"], TILES)
            mm(t_b[:, 0:EXPERTS], ones[:, :], mask_sum[:, :], start=True, stop=False)
            mm(t_b[:, 0:EXPERTS], ones[:, :], mask_bf[:, :], start=False, stop=True).then_inc(s["count_ps"], 1)
            pe.wait_ge(s["split_lo"], SPLIT_STEPS)
            pe.wait_ge(s["table_step"], TABLE_TILES)

            def rows_transposed(j, par):
                pe.wait_ge(b_in[par], (j - par) * 8 + 16)
                need(pe, s["b_x_low"], j)
                transposed(q_b, list_rows[:, cols(par)]).then_inc(s["b_t_ps"], 1)

            def expert_of(j):
                return pe.value_load(expert_i[0:1, bass.ds(j, 1)], min_val=0, max_val=EXPERTS - 1)

            def gate_up(j, par, expert):
                pe.wait_ge(s["b_x_low"], j + 1)
                for kt in range(KT):
                    last = product(h_b, [t[:, par * DIM + kt * P:par * DIM + (kt + 1) * P] for t in (x2_hi, x2_lo)],
                                   [t[:, bass.ds(expert * EW + kt * UP, UP)] for t in (w_hi, w_lo)],
                                   start=kt == 0, stop=kt == KT - 1)
                last.then_inc(s["b_h_ps"], 1)

            def step_b(j, par, known):
                if known is None or known + 2 < TILES_B:
                    rows_transposed(j + 2, par)
                pe.wait_ge(s["b_hid"], j + 1)
                transposed(t_b, hid).then_inc(s["b_ht_ps"], 1)
                if known is None or known + 1 < TILES_B:
                    gate_up(j + 1, 1 - par, expert_of(j + 1))
                expert = expert_of(j)
                pe.wait_ge(s["b_h_low"], j + 1)
                need(pe, s["b_y"], j)
                for kt in range(KT):
                    last = product(o_b[:, 0:DIM], [t[:, cols(kt, P)] for t in (h_hi, h_lo)],
                                   [t[:, bass.ds(expert * EW + KT * UP + kt * DIM, DIM)] for t in (w_hi, w_lo)],
                                   start=kt == 0, stop=kt == KT - 1)
                last.then_inc(s["b_y_ps"], 1)

            rows_transposed(0, 0)
            rows_transposed(1, 1)
            gate_up(0, 0, expert_of(0))
            run_phase_b(pe, step_b)


_OUT = ((BATCH, SEQ, DIM), "float32")


def _partition_first(w_t):
    n = w_t.shape[-1]
    return np.ascontiguousarray(w_t.reshape(KT, P, n).transpose(1, 0, 2).reshape(P, KT * n))


def kernel(**inputs):
    import concourse.bacc as bacc
    from concourse.bass_utils import run_bass_kernel_spmd

    a = {k.removeprefix("L0_"): np.asarray(v) for k, v in inputs.items()}
    x = np.ascontiguousarray(a["x"].reshape(TOKENS, DIM))
    ctx = np.tile(a["ctx_1024"].transpose(2, 0, 1), (1, 1, 3)).reshape(DIM, BATCH * 3 * KEYS)

    def expert(w1, w3, w2):
        up = _partition_first(np.concatenate([w1.T, w3.T], axis=1))
        return np.concatenate([up, _partition_first(w2.T)], axis=1)

    experts = [expert(a["ffn_w1"][e], a["ffn_w3"][e], a["ffn_w2"][e]) for e in range(EXPERTS)]
    shared = expert(a["ffn_sw1"], a["ffn_sw3"], a["ffn_sw2"])
    arrays = {
        "in_x": x,
        "in_ctx": _partition_first(ctx),
        "in_wq": _partition_first(a["xattn_w_q"].T),
        "in_wk": _partition_first(a["xattn_w_k"].T),
        "in_wv": _partition_first(a["xattn_w_v"].T),
        "in_wo": _partition_first(a["xattn_w_o"].T),
        "in_gate": _partition_first(a["ffn_gate_w"].T),
        "in_bias": np.ascontiguousarray(a["ffn_expert_bias"]),
        "in_ffn": np.ascontiguousarray(np.concatenate(experts + [shared], axis=1)),
    }
    nc = bacc.Bacc("TRN2", target_bir_lowering=False, num_devices=1)
    args = [nc.dram_tensor(n, v.shape, mybir.dt.from_np(v.dtype), kind="ExternalInput").ap()
            for n, v in arrays.items()]
    out = nc.dram_tensor("out_x", (TOKENS, DIM), mybir.dt.from_np(np.dtype(_OUT[1])), kind="ExternalOutput").ap()
    layer_kernel(nc, *args, out)
    r = run_bass_kernel_spmd(nc, [arrays], core_ids=[0])
    return r.results[0]["out_x"].reshape(_OUT[0])
```

```python
import numpy as np
import concourse.bass as bass
from concourse import mybir

F32 = mybir.dt.float32
F32R = mybir.dt.float32r
BF16 = mybir.dt.bfloat16
I32 = mybir.dt.int32
U32 = mybir.dt.uint32
ALU = mybir.AluOpType
ACT = mybir.ActivationFunctionType
AXX = mybir.AxisListType.X

P = 128
BATCH, SEQ, DIM = 2, 1024, 256
KEYS, HEADS = 77, 16
HD = DIM // HEADS
TOKENS = BATCH * SEQ
TILES = TOKENS // P
TILES_PER_BATCH = SEQ // P
KT = DIM // P
EXPERTS, TOPK = 8, 2
EPS = 1e-5
BANK = 512
HEADS_PER_BANK = 4
BANK_COLS = HEADS_PER_BANK * KEYS
HALF_COLS = HEADS * KEYS // 2
CHUNKS = -(-HEADS * KEYS // P)
PCOLS = CHUNKS * P
VHEADS = 3
VN = CHUNKS * VHEADS
HV = HD + 1
UP = 2 * DIM
EW = KT * UP + KT * DIM
REGION = TOKENS + P
ROW = DIM + 3
ID_EVEN, SCORE, ID_ODD = DIM, DIM + 1, DIM + 2
RESULTS = TOPK * TOKENS
TILES_B = TOPK * TOKENS // P + EXPERTS - 1
SPLIT_STEPS = 12
SPLIT = EXPERTS * EW // SPLIT_STEPS
SUM_BUFS = 4

FIRST, LAST = -2, TILES + 3
ROUTE_LINKS, ROUTE_SCORES = 10, 8
TABLE_COUNTS, TABLE_TILES = 2, 15


def head_base(c):
    return min(P * c // KEYS, HEADS - VHEADS)


def need(eng, semaphore, value):
    if not isinstance(value, int) or value > 0:
        eng.wait_ge(semaphore, value)


def live(known, shift):
    return known is None or 0 <= known + shift < TILES


def splitting(known):
    return known is None or 2 <= known < 2 + SPLIT_STEPS


def run_phase_a(eng, step):
    for i in range(FIRST, 4):
        step(i, i % 2, i, 0)
    for batch, (lo, hi) in enumerate(((4, TILES_PER_BATCH), (TILES_PER_BATCH, TILES - 2))):
        with eng.Fori(lo // 2, hi // 2) as turn:
            for par in range(2):
                step(turn * 2 + par, par, None, batch)
    for i in range(TILES - 2, LAST):
        step(i, i % 2, i, 1)


def run_phase_b(eng, step):
    for j in range(2):
        step(j, j, j)
    with eng.Fori(1, (TILES_B - 3) // 2) as turn:
        for par in range(2):
            step(turn * 2 + par, par, None)
    for j in range(TILES_B - 3, TILES_B):
        step(j, j % 2, j)


def cols(n, width=DIM):
    return bass.ds(n * width, width)


def v3(t, a):
    return t.rearrange("p (a b) -> p a b", a=a)


def layer_kernel(nc, x, ctxt, wqt, wkt, wvt, wot, gatet, bias, wffn, out):
    def sb(name, n, dt=F32):
        return nc.alloc_sbuf_tensor(name, [P, n], dt)

    lists = nc.dram_tensor("lists", [EXPERTS * REGION + P, ROW], F32, kind="Internal").ap()
    results = nc.dram_tensor("results", [RESULTS + 2 * P, DIM], F32, kind="Internal").ap()

    resid = sb("resid", TILES * DIM)
    wq, wk, wv, wo = (sb(n, KT * DIM) for n in ("wq", "wk", "wv", "wo"))
    gate_raw = sb("gate_raw", KT * EXPERTS)
    gate_hi = sb("gate_hi", KT * EXPERTS, F32R)
    gate_lo = sb("gate_lo", KT * EXPERTS, F32R)
    bias_b = sb("bias_b", EXPERTS)
    ctx_t = sb("ctx_t", KT * BATCH * 3 * KEYS)
    w_stage = sb("w_stage", 2 * SPLIT)
    w_hi = sb("w_hi", (EXPERTS + 1) * EW, F32R)
    w_lo = sb("w_lo", (EXPERTS + 1) * EW, F32R)
    k_raw = sb("k_raw", 2 * BATCH * KEYS)
    k_raw_hi = sb("k_raw_hi", 2 * BATCH * KEYS, F32R)
    k_raw_lo = sb("k_raw_lo", 2 * BATCH * KEYS, F32R)
    k_hi = sb("k_hi", BATCH * 2 * BANK_COLS, F32R)
    k_lo = sb("k_lo", BATCH * 2 * BANK_COLS, F32R)
    vals = sb("vals", BATCH * VN * HV)
    ident = sb("ident", P)
    head_of, head_mask = sb("head_of", 2 * HEADS_PER_BANK), sb("head_mask", HEADS_PER_BANK)
    val_mask = sb("val_mask", VN)
    upper = sb("upper", P, BF16)
    ones = sb("ones", P, BF16)
    minus_half = sb("minus_half", 1)
    iota_e = sb("iota_e", EXPERTS)
    iota_m = sb("iota_m", TILES)
    iota_j = sb("iota_j", TILES_B)
    ones_e = sb("ones_e", EXPERTS)
    pad_rows = sb("pad_rows", ROW)
    ids = sb("ids", TILES * TOPK, I32)
    stats1, mv1, ve1, rstd1 = sb("stats1", 6), sb("mv1", 2), sb("ve1", 1), sb("rstd1", 1)
    stats2, mv2, ve2, rstd2 = sb("stats2", 6), sb("mv2", 2), sb("ve2", 1), sb("rstd2", 1)
    xn, xn_t = sb("xn", DIM), sb("xn_t", DIM)
    q_hi, q_lo = sb("q_hi", DIM, F32R), sb("q_lo", DIM, F32R)
    row_max, row_inv = sb("row_max", HEADS), sb("row_inv", HEADS)
    shared_space = sb("shared_space", 2 * PCOLS)
    probs, probs_t = shared_space[:, 0:PCOLS], shared_space[:, PCOLS:2 * PCOLS]
    sum_rows = shared_space[:, 0:SUM_BUFS * TOPK * DIM]
    attn, attn_t = sb("attn", DIM), sb("attn_t", DIM)
    xn2 = sb("xn2", 2 * (DIM + 1))
    x2_hi, x2_lo = sb("x2_hi", 2 * DIM, F32R), sb("x2_lo", 2 * DIM, F32R)
    act_s, silu_s, hid = sb("act_s", DIM), sb("silu_s", DIM), sb("hid", DIM)
    h_hi, h_lo = sb("h_hi", DIM, F32R), sb("h_lo", DIM, F32R)
    th8, score, ranked, top8 = (sb(n, EXPERTS) for n in ("th8", "score", "ranked", "top8"))
    top8_i = sb("top8_i", EXPERTS, U32)
    chosen_f = sb("chosen_f", TOPK)
    picked = sb("picked", TOPK * EXPERTS)
    mask_bf, mask_sum = sb("mask_bf", EXPERTS, BF16), sb("mask_sum", EXPERTS, BF16)
    onehot, picked_r = sb("onehot", 2 * TOPK * EXPERTS), sb("picked_r", TOPK * EXPERTS)
    scores2, ranks2 = sb("scores2", TILES * TOPK), sb("ranks2", TOPK)
    dest_f, dest = sb("dest_f", TOPK), sb("dest", 2 * TOPK, I32)
    scaled = sb("scaled", 2 * TOPK * ROW)
    counts, counts_i = sb("counts", EXPERTS), sb("counts_i", EXPERTS, I32)
    over = sb("over", EXPERTS * TILES)
    n_tiles, end_tile, start_tile = (sb(n, EXPERTS) for n in ("n_tiles", "end_tile", "start_tile"))
    passed, passed_n = sb("passed", TILES_B * EXPERTS), sb("passed_n", TILES_B * EXPERTS)
    expert_f, before_f, row_f = (sb(n, TILES_B) for n in ("expert_f", "before_f", "row_f"))
    expert_i, row_i = sb("expert_i", TILES_B, I32), sb("row_i", TILES_B, I32)
    list_rows, y_rows = sb("list_rows", 2 * ROW), sb("y_rows", 2 * DIM)
    meta, y_meta = sb("meta", 2 * 2), sb("y_meta", 2 * 2)

    psum = nc.alloc_psum_tensor("psum", [P, 8 * BANK], F32)
    bank = [psum[:, n * BANK:(n + 1) * BANK] for n in range(8)]
    o_b, q_b, t_b, h_b = bank[4:8]
    score_view = (psum[:, 0:4 * BANK].rearrange("p (g c) -> p g c", g=4)[:, :, 0:BANK_COLS]
                  .rearrange("p g (h k) -> p g h k", k=KEYS))

    s = {name: nc.alloc_semaphore(name) for name in (
        "x0_in x_in ctx_in wk_in wq_in wv_in wo_in gate_in bias_in shared_in split_in0 split_in1 "
        "filled masked pads_done k_ps k_out k_low k_masked v_ps v_done gate_high gate_low "
        "shared_hi shared_lo split_hi split_lo "
        "ln1_step pow1 xn1 t1_ps t1_out q_ps q_high q_low s_ps maxed subbed exped pt_ps pt_out "
        "pv_ps inv_done normed ot_ps ot_out o_ps x1_done ln2_step pow2 xn2_done "
        "t2_ps x2_high x2_low h_ps tanh_h silu_done hid_done gate_ps tanh_g route_step scaled_done "
        "rank_ps rank_read scat0 scat1 ht_ps h_high h_low y_ps acc_done count_ps table_step dest_step pad_out "
        "b_in0 b_in1 b_t_ps b_x_high b_x_low b_h_ps b_silu b_hid b_ht_ps b_h_high b_h_low b_y_ps "
        "b_y b_meta b_y_meta b_out0 b_out1 c_in0 c_in1 c_in2 c_in3 c_first c_sum c_out").split()}
    split_in, scat = [s["split_in0"], s["split_in1"]], [s["scat0"], s["scat1"]]
    b_in, b_out = [s["b_in0"], s["b_in1"]], [s["b_out0"], s["b_out1"]]
    c_in = [s[f"c_in{n}"] for n in range(SUM_BUFS)]

    with nc.Block() as block:

        @block.sync
        def _(sp):
            sp.dma_start(ctx_t[:, :], ctxt).then_inc(s["ctx_in"], 16)
            sp.dma_start(wk[:, :], wkt).then_inc(s["wk_in"], 16)
            x_tiles = x.rearrange("(t p) d -> p t d", p=P)
            resid_tiles = resid[:, :].rearrange("p (t d) -> p t d", d=DIM)
            sp.dma_start(resid_tiles[:, 0:2, :], x_tiles[:, 0:2, :]).then_inc(s["x0_in"], 16)
            sp.dma_start(wv[:, :], wvt).then_inc(s["wv_in"], 16)
            sp.dma_start(wo[:, :], wot).then_inc(s["wo_in"], 16)
            for a in (2, 9):
                sp.dma_start(resid_tiles[:, a:a + 7, :], x_tiles[:, a:a + 7, :]).then_inc(s["x_in"], 16)

            sp.dma_start(w_stage[:, 0:EW], wffn[:, EXPERTS * EW:(EXPERTS + 1) * EW]).then_inc(s["shared_in"], 16)
            sp.wait_ge(s["shared_lo"], 1)
            for n in range(2):
                sp.dma_start(w_stage[:, n * SPLIT:(n + 1) * SPLIT],
                             wffn[:, n * SPLIT:(n + 1) * SPLIT]).then_inc(split_in[n], 16)
            with sp.Fori(0, SPLIT_STEPS // 2 - 1) as turn:
                for par in range(2):
                    sp.wait_ge(s["split_lo"], turn * 2 + par + 1)
                    sp.dma_start(w_stage[:, cols(par, SPLIT)],
                                 wffn[:, cols(turn * 2 + par + 2, SPLIT)]).then_inc(split_in[par], 16)

            sp.wait_ge(s["table_step"], TABLE_COUNTS)
            sp.wait_ge(s["pads_done"], 5)
            for e in range(EXPERTS):
                n_rows = sp.value_load(counts_i[0:1, e:e + 1], min_val=0, max_val=TOKENS)
                sp.dma_start(lists[bass.ds(n_rows + e * REGION, P), :], pad_rows[:, :]).then_inc(s["pad_out"], 16)
            sp.dma_start(lists[EXPERTS * REGION:, :], pad_rows[:, :]).then_inc(s["pad_out"], 16)
            sp.wait_ge(s["pad_out"], 16 * (EXPERTS + 1))
            for par in range(2):
                sp.wait_ge(scat[par], 16 * TOPK * (TILES // 2))
            sp.wait_ge(s["table_step"], TABLE_TILES)

            def load(j, par):
                row = sp.value_load(row_i[0:1, bass.ds(j, 1)], min_val=0, max_val=EXPERTS * REGION)
                sp.dma_start(list_rows[:, cols(par, ROW)], lists[bass.ds(row, P), :]).then_inc(b_in[par], 16)

            for j in range(2):
                load(j, j)
            with sp.Fori(1, (TILES_B - 1) // 2) as turn:
                for par in range(2):
                    sp.wait_ge(s["b_t_ps"], turn * 2 + par - 1)
                    sp.wait_ge(s["b_meta"], turn * 2 + par - 1)
                    load(turn * 2 + par, par)
            sp.wait_ge(s["b_t_ps"], TILES_B - 2)
            sp.wait_ge(s["b_meta"], TILES_B - 2)
            load(TILES_B - 1, (TILES_B - 1) % 2)

            for par in range(2):
                sp.wait_ge(b_out[par], 16 * ((TILES_B + 1 - par) // 2))
            token_rows = results[0:RESULTS, :].rearrange("(t k) d -> t (k d)", k=TOPK)
            for n in range(SUM_BUFS):
                sp.dma_start(sum_rows[:, cols(n, TOPK * DIM)], token_rows[cols(n, P), :]).then_inc(c_in[n], 16)
            with sp.Fori(1, TILES // SUM_BUFS) as turn:
                for n in range(SUM_BUFS):
                    t = turn * SUM_BUFS + n
                    sp.wait_ge(s["c_sum"], t - SUM_BUFS + 1)
                    sp.dma_start(sum_rows[:, cols(n, TOPK * DIM)], token_rows[cols(t, P), :]).then_inc(c_in[n], 16)

        @block.gpsimd
        def _(pool):
            fills = ((ident, 0.0), (head_of, 1.0), (val_mask, 1.0), (upper, 1.0), (ones, 1.0),
                     (minus_half, -0.5), (mask_sum, 0.0), (mask_bf, 0.0), (ones_e, 1.0))
            once = ((pad_rows, 0, ROW, 0.0), (xn2, DIM, DIM + 1, 1.0), (xn2, 2 * DIM + 1, 2 * DIM + 2, 1.0))
            for t, value in fills:
                pool.memset(t[:, :], value).then_inc(s["filled"], 1)
            pool.memset(probs[:, HEADS * KEYS:PCOLS], 0.0).then_inc(s["filled"], 1)
            for t, pitch, n in ((iota_e, 1, EXPERTS), (iota_m, P, TILES), (iota_j, 1, TILES_B)):
                pool.iota(t[:, :], pattern=[[pitch, n]], base=0, channel_multiplier=0,
                          allow_small_or_imprecise_dtypes=True).then_inc(s["filled"], 1)
            pool.wait_ge(s["filled"], 13)

            def cut(t, op, fill, base, pattern, per_partition):
                pool.affine_select(out=t, in_=t, compare_op=op, fill=fill, base=base, pattern=[pattern],
                                   channel_multiplier=per_partition).then_inc(s["masked"], 1)

            cut(ident[:, :], ALU.not_equal, 1.0, 0, [-1, P], 1)
            cut(head_of[:, :], ALU.is_ge, 0.0, 0, [-HD, 2 * HEADS_PER_BANK], 1)
            pool.wait_ge(s["masked"], 2)
            cut(head_of[:, :], ALU.is_ge, 0.0, HD - 1, [HD, 2 * HEADS_PER_BANK], -1)
            pool.wait_ge(s["masked"], 3)
            pool.tensor_tensor(head_mask[:, :], head_of[:, 0:HEADS_PER_BANK], head_of[:, HEADS_PER_BANK:],
                               ALU.add).then_inc(s["masked"], 1)
            for c in range(CHUNKS):
                cut(val_mask[:, cols(c, VHEADS)], ALU.is_ge, 0.0, P * c - KEYS * head_base(c),
                    [-KEYS, VHEADS], 1)
            pool.wait_ge(s["masked"], 4 + CHUNKS)
            for c in range(CHUNKS):
                cut(val_mask[:, cols(c, VHEADS)], ALU.is_ge, 0.0, KEYS * head_base(c) + KEYS - 1 - P * c,
                    [KEYS, VHEADS], -1)
            cut(upper[:, :], ALU.is_ge, 0.0, -1, [1, P], -1)
            for t, a, b, value in once:
                pool.memset(t[:, a:b], value).then_inc(s["pads_done"], 1)
            pool.wait_ge(s["pads_done"], 3)
            for a, extra in ((ID_EVEN, 0), (ID_ODD, P)):
                pool.iota(pad_rows[:, a:a + 1].bitcast(I32), pattern=[[0, 1]], base=RESULTS + extra,
                          channel_multiplier=1).then_inc(s["pads_done"], 1)
            pool.iota(ids[:, :], pattern=[[P * TOPK, TILES], [1, TOPK]], base=0,
                      channel_multiplier=TOPK).then_inc(s["pads_done"], 1)

            def scatter(par):
                for k in range(TOPK):
                    n = par * TOPK + k
                    pool.indirect_dma_start(
                        lists, bass.IndirectOffsetOnAxis(ap=dest[:, n:n + 1], axis=0),
                        scaled[:, cols(n, ROW)], None).then_inc(scat[par], 16)

            def step(i, par, known, _):
                if live(known, -1):
                    pool.wait_ge(s["ln2_step"], 3 * i)
                    pool.tensor_tensor(rstd2[:, :], ve2[:, :], minus_half[:, :], ALU.pow).then_inc(s["pow2"], 1)
                if live(known, -3):
                    pool.wait_ge(s["scaled_done"], 3 * TOPK * (i - 2))
                    pool.wait_ge(s["dest_step"], 3 * (i - 2))
                if live(known, 2):
                    pool.wait_ge(s["ln1_step"], 3 * (i + 3))
                    pool.tensor_tensor(rstd1[:, :], ve1[:, :], minus_half[:, :], ALU.pow).then_inc(s["pow1"], 1)
                if live(known, -3):
                    scatter(1 - par)
                if known == -1:
                    pool.wait_ge(s["shared_hi"], 1)
                    pool.tensor_tensor(w_lo[:, cols(EXPERTS, EW)], w_stage[:, 0:EW],
                                       w_hi[:, cols(EXPERTS, EW)].bitcast(F32),
                                       ALU.subtract).then_inc(s["shared_lo"], 1)
                if splitting(known):
                    pool.wait_ge(s["split_hi"], i - 1)
                    pool.tensor_tensor(w_lo[:, cols(i - 2, SPLIT)], w_stage[:, cols(par, SPLIT)],
                                       w_hi[:, cols(i - 2, SPLIT)].bitcast(F32),
                                       ALU.subtract).then_inc(s["split_lo"], 1)
                if live(known, -2):
                    if known == 2:
                        pool.wait_ge(s["pads_done"], 6)
                    pool.wait_ge(s["route_step"], (i - 2) * ROUTE_LINKS + ROUTE_SCORES)
                    need(pool, scat[par], (i - 2 - par) * 8 * TOPK)
                    for k in range(TOPK):
                        n = par * TOPK + k
                        a = n * ROW
                        score_k = scores2[:, cols((i - 2) * TOPK + k, 1)]
                        xs = xn2[:, cols(par, DIM + 1)]
                        pool.tensor_tensor(scaled[:, a:a + DIM], xs[:, 0:DIM],
                                           score_k.to_broadcast([P, DIM]), ALU.mult).then_inc(s["scaled_done"], 1)
                        pool.tensor_tensor(scaled[:, a + SCORE:a + SCORE + 1], xs[:, DIM:DIM + 1],
                                           score_k, ALU.mult).then_inc(s["scaled_done"], 1)
                        id_k = ids[:, cols((i - 2) * TOPK + k, 1)]
                        pool.tensor_copy(scaled[:, a + ID_EVEN:a + ID_ODD + 1:2].bitcast(I32),
                                         id_k.to_broadcast([P, 2])).then_inc(s["scaled_done"], 1)

            run_phase_a(pool, step)

            for j in range(TILES_B):
                par = j % 2
                pool.wait_ge(s["b_y"], j + 1)
                pool.wait_ge(s["b_y_meta"], j + 1)
                index = y_meta[:, 2 * par + par:2 * par + par + 1].bitcast(I32)
                pool.indirect_dma_start(
                    results, bass.IndirectOffsetOnAxis(ap=index, axis=0),
                    y_rows[:, cols(par)], None).then_inc(b_out[par], 16)

        @block.scalar
        def _(act):
            act.dma_start(wq[:, :], wqt).then_inc(s["wq_in"], 16)
            act.dma_start(gate_raw[:, :], gatet).then_inc(s["gate_in"], 16)
            act.dma_start(bias_b[:, :], bias.partition_broadcast(P)).then_inc(s["bias_in"], 16)
            act.wait_ge(s["k_ps"], 1)
            act.activation(k_raw[:, :], h_b[:, 0:2 * BATCH * KEYS], ACT.Copy).then_inc(s["k_out"], 1)
            act.wait_ge(s["k_out"], 1)
            act.activation(k_raw_hi[:, :], k_raw[:, :], ACT.Copy).then_inc(s["k_out"], 1)
            act.wait_ge(s["gate_in"], 16)
            act.activation(gate_hi[:, :], gate_raw[:, :], ACT.Copy).then_inc(s["gate_high"], 1)

            def step(i, par, known, _):
                if live(known, 1):
                    act.wait_ge(s["t1_ps"], i + 2)
                    act.activation(xn_t[:, :], q_b[:, 0:DIM], ACT.Copy).then_inc(s["t1_out"], 1)
                if live(known, -2):
                    act.wait_ge(s["t2_ps"], i - 1)
                    act.activation(x2_hi[:, 0:DIM], t_b[:, 0:DIM], ACT.Copy).then_inc(s["x2_high"], 1)
                if live(known, 1):
                    act.wait_ge(s["q_ps"], i + 2)
                    act.activation(q_hi[:, :], q_b[:, 0:DIM], ACT.Copy).then_inc(s["q_high"], 1)
                if live(known, 0):
                    for g in range(2):
                        act.wait_ge(s["subbed"], 2 * i + g + 1)
                        part = probs[:, cols(g, HALF_COLS)]
                        act.activation(part, part, ACT.Exp, scale=float(HD) ** -0.5).then_inc(s["exped"], 1)
                if live(known, -2):
                    act.wait_ge(s["h_ps"], i - 1)
                    need(act, s["silu_done"], i - 2)
                    act.activation(act_s[:, :], h_b[:, 0:DIM], ACT.Tanh, scale=0.5).then_inc(s["tanh_h"], 1)
                    act.wait_ge(s["gate_ps"], i - 1)
                    act.activation(th8[:, :], t_b[:, 0:EXPERTS], ACT.Tanh, scale=0.5).then_inc(s["tanh_g"], 1)
                if live(known, 0):
                    for g in range(3):
                        act.wait_ge(s["pt_ps"], 3 * i + g + 1)
                        n = min(BANK, PCOLS - BANK * g)
                        act.activation(probs_t[:, BANK * g:BANK * g + n], bank[g][:, 0:n],
                                       ACT.Copy).then_inc(s["pt_out"], 1)
                if live(known, -2):
                    act.wait_ge(s["ht_ps"], i - 1)
                    act.activation(h_hi[:, :], t_b[:, 0:DIM], ACT.Copy).then_inc(s["h_high"], 1)
                if splitting(known):
                    act.wait_ge(split_in[par], (i - par) * 8)
                    act.activation(w_hi[:, cols(i - 2, SPLIT)], w_stage[:, cols(par, SPLIT)],
                                   ACT.Copy).then_inc(s["split_hi"], 1)
                if known == -1:
                    act.wait_ge(s["shared_in"], 16)
                    act.activation(w_hi[:, cols(EXPERTS, EW)], w_stage[:, 0:EW], ACT.Copy).then_inc(s["shared_hi"], 1)
                if live(known, 0):
                    act.wait_ge(s["ot_ps"], i + 1)
                    act.activation(attn_t[:, :], q_b[:, 0:DIM], ACT.Copy).then_inc(s["ot_out"], 1)

            run_phase_a(act, step)

            def x_high(j, par):
                act.wait_ge(s["b_t_ps"], j + 1)
                act.activation(x2_hi[:, cols(par)], q_b[:, 0:DIM], ACT.Copy).then_inc(s["b_x_high"], 1)

            def silu(j):
                act.wait_ge(s["b_h_ps"], j + 1)
                need(act, s["b_hid"], j)
                act.activation(act_s[:, :], h_b[:, 0:DIM], ACT.Silu).then_inc(s["b_silu"], 1)

            def step_b(j, par, known):
                if known is None or known + 2 < TILES_B:
                    x_high(j + 2, par)
                act.wait_ge(s["b_ht_ps"], j + 1)
                act.activation(h_hi[:, :], t_b[:, 0:DIM], ACT.Copy).then_inc(s["b_h_high"], 1)
                if known is None or known + 1 < TILES_B:
                    silu(j + 1)
                act.wait_ge(s["b_y_ps"], j + 1)
                act.wait_ge(s["b_y_meta"], j + 1)
                act.activation(y_rows[:, cols(par)], o_b[:, 0:DIM], ACT.Copy,
                               scale=y_meta[:, 2 * par + 1 - par:2 * par + 2 - par]).then_inc(s["b_y"], 1)

            x_high(0, 0)
            x_high(1, 1)
            silu(0)
            run_phase_b(act, step_b)

            with act.Fori(0, TILES) as t:
                act.wait_ge(s["c_sum"], t + 1)
                act.dma_start(out[cols(t, P), :], resid[:, cols(t)]).then_inc(s["c_out"], 16)
            act.wait_ge(s["c_out"], 16 * TILES)

        @block.vector
        def _(dve):
            tt, stt, ts = dve.tensor_tensor, dve.scalar_tensor_tensor, dve.tensor_scalar

            def chain(semaphore, before):
                count = [0]

                def link(ins, until=True):
                    count[0] += 1
                    ins.then_inc(semaphore, 1)
                    if until:
                        dve.wait_ge(semaphore, before + count[0])
                return link

            def values(b, source):
                dve.wait_ge(s["v_ps"], b + 1)
                view = v3(vals[:, cols(b, VN * HV)], VN)
                tt(view[:, :, 0:HD], v3(source[:, 0:VN * HD], VN),
                   val_mask[:, :].unsqueeze(2).to_broadcast([P, VN, HD]), ALU.mult).then_inc(s["v_done"], 1)
                dve.tensor_copy(view[:, :, HD:HV], val_mask[:, :].unsqueeze(2)).then_inc(s["v_done"], 1)

            dve.wait_ge(s["k_out"], 2)
            tt(k_raw_lo[:, :], k_raw[:, :], k_raw_hi[:, :].bitcast(F32), ALU.subtract).then_inc(s["k_low"], 1)
            dve.wait_ge(s["masked"], 4)
            dve.wait_ge(s["k_low"], 1)

            def keys(b):
                for half in range(2):
                    for raw, part in ((k_raw_hi, k_hi), (k_raw_lo, k_lo)):
                        tt(v3(part[:, cols(b * 2 + half, BANK_COLS)], HEADS_PER_BANK),
                           raw[:, cols(half * BATCH + b, KEYS)].bitcast(F32).unsqueeze(1)
                           .to_broadcast([P, HEADS_PER_BANK, KEYS]),
                           head_mask[:, :].unsqueeze(2).to_broadcast([P, HEADS_PER_BANK, KEYS]),
                           ALU.mult).then_inc(s["k_masked"], 1)

            def step(i, par, known, _):
                if live(known, -3):
                    place = chain(s["dest_step"], (i - 3) * 3)
                    ranks = ranks2[:, :]
                    dve.wait_ge(s["rank_ps"], i - 2)
                    tt(v3(picked_r[:, :], TOPK), v3(onehot[:, cols(1 - par, TOPK * EXPERTS)], TOPK),
                       t_b[:, 0:EXPERTS].unsqueeze(1).to_broadcast([P, TOPK, EXPERTS]),
                       ALU.mult).then_inc(s["rank_read"], 1)
                if live(known, 0):
                    dve.wait_ge(s["s_ps"], i + 1)
                    dve.tensor_reduce(v3(row_max[:, :], 4), score_view, axis=AXX, op=ALU.max).then_inc(s["maxed"], 1)
                if live(known, -3):
                    dve.wait_ge(s["rank_read"], i - 2)
                    place(dve.tensor_reduce(ranks, v3(picked_r[:, :], TOPK), axis=AXX, op=ALU.add), until=False)
                if live(known, -1):
                    dve.wait_ge(s["o_ps"], i)
                    x1 = resid[:, cols(i - 1)]
                    tt(x1, x1, o_b[:, 0:DIM], ALU.add).then_inc(s["x1_done"], 1)
                if live(known, -3):
                    dve.wait_ge(s["dest_step"], (i - 3) * 3 + 1)
                    place(stt(dest_f[:, :], chosen_f[:, :], float(REGION), ranks, ALU.mult, ALU.add), until=False)
                if live(known, -2):
                    dve.wait_ge(s["x2_high"], i - 1)
                    tt(x2_lo[:, 0:DIM], t_b[:, 0:DIM], x2_hi[:, 0:DIM].bitcast(F32),
                       ALU.subtract).then_inc(s["x2_low"], 1)
                if live(known, -3):
                    dve.wait_ge(s["dest_step"], (i - 3) * 3 + 2)
                    dve.wait_ge(s["scaled_done"], 3 * TOPK * (i - 2))
                    place(dve.tensor_copy(dest[:, cols(1 - par, TOPK)], dest_f[:, :]), until=False)
                if live(known, 0):
                    dve.wait_ge(s["maxed"], i + 1)
                    for g in range(2):
                        tt(probs[:, cols(g, HALF_COLS)].rearrange("p (b h k) -> p b h k", b=2, k=KEYS),
                           score_view[:, 2 * g:2 * g + 2, :, :],
                           v3(row_max[:, cols(g, HEADS // 2)], 2).unsqueeze(3)
                           .to_broadcast([P, 2, HEADS_PER_BANK, KEYS]), ALU.subtract).then_inc(s["subbed"], 1)
                if live(known, -1):
                    dve.wait_ge(s["x1_done"], i)
                if live(known, 1):
                    dve.wait_ge(s["q_high"], i + 2)
                    tt(q_lo[:, :], q_b[:, 0:DIM], q_hi[:, :].bitcast(F32), ALU.subtract).then_inc(s["q_low"], 1)
                norms = []
                if live(known, -1):
                    norms.append((s["ln2_step"], (i - 1) * 3, stats2, mv2, ve2, x1))
                if live(known, 2):
                    if known == FIRST:
                        dve.wait_ge(s["x0_in"], 16)
                    if known == 0:
                        dve.wait_ge(s["x_in"], 32)
                    x0 = resid[:, cols(i + 2)]
                    norms.append((s["ln1_step"], (i + 2) * 3, stats1, mv1, ve1, x0))
                for done, before, st, mv, ve, rows in norms:
                    dve.bn_stats(st[:, :], rows).then_inc(done, 1)
                for done, before, st, mv, ve, rows in norms:
                    dve.wait_ge(done, before + 1)
                if live(known, -2):
                    dve.wait_ge(s["tanh_h"], i - 1)
                    stt(silu_s[:, :], act_s[:, :], 1.0, h_b[:, 0:DIM], ALU.add, ALU.mult).then_inc(s["silu_done"], 1)
                for done, before, st, mv, ve, rows in norms:
                    dve.bn_aggr(mv[:, :], st[:, :]).then_inc(done, 1)
                if live(known, -2):
                    dve.wait_ge(s["silu_done"], i - 1)
                    stt(hid[:, :], silu_s[:, :], 0.5, h_b[:, DIM:2 * DIM], ALU.mult, ALU.mult).then_inc(s["hid_done"], 1)
                for done, before, st, mv, ve, rows in norms:
                    dve.wait_ge(done, before + 2)
                    ts(ve[:, :], mv[:, 1:2], EPS, None, ALU.add).then_inc(done, 1)
                if live(known, -2):
                    link = chain(s["route_step"], (i - 2) * ROUTE_LINKS)
                    hot = onehot[:, cols(par, TOPK * EXPERTS)]
                    hot0, hot1 = hot[:, 0:EXPERTS], hot[:, EXPERTS:]
                    dve.wait_ge(s["tanh_g"], i - 1)
                    link(ts(score[:, :], th8[:, :], 0.5, 0.5, ALU.mult, ALU.add))
                    link(tt(ranked[:, :], score[:, :], bias_b[:, :], ALU.add))
                if live(known, -1):
                    dve.wait_ge(s["pow2"], i)
                    need(dve, s["scaled_done"], 3 * TOPK * (i - 2))
                    ts(xn2[:, (1 - par) * (DIM + 1):(1 - par) * (DIM + 1) + DIM], x1, mv2[:, 0:1], rstd2[:, :],
                       ALU.subtract, ALU.mult).then_inc(s["xn2_done"], 1)
                if live(known, -2):
                    link(dve.max(top8[:, :], ranked[:, :]), until=False)
                if live(known, -2):
                    dve.wait_ge(s["route_step"], (i - 2) * ROUTE_LINKS + 3)
                    dve.wait_ge(s["h_high"], i - 1)
                    tt(h_lo[:, :], t_b[:, 0:DIM], h_hi[:, :].bitcast(F32), ALU.subtract).then_inc(s["h_low"], 1)
                if live(known, -2):
                    link(dve.max_index(top8_i[:, :], top8[:, :], ranked[:, :]), until=False)
                if live(known, 2):
                    dve.wait_ge(s["pow1"], i + 3)
                    need(dve, s["t1_ps"], i + 2)
                    ts(xn[:, :], x0, mv1[:, 0:1], rstd1[:, :], ALU.subtract, ALU.mult).then_inc(s["xn1"], 1)
                if live(known, -2):
                    dve.wait_ge(s["route_step"], (i - 2) * ROUTE_LINKS + 4)
                    link(dve.tensor_copy(chosen_f[:, :], top8_i[:, 0:TOPK]))
                    link(tt(v3(hot, TOPK), iota_e[:, :].unsqueeze(1).to_broadcast([P, TOPK, EXPERTS]),
                            chosen_f[:, :].unsqueeze(2).to_broadcast([P, TOPK, EXPERTS]), ALU.is_equal), until=False)
                if live(known, 0):
                    dve.wait_ge(s["pv_ps"], i + 1)
                    o_heads = v3(o_b[:, 0:HEADS * HV], HEADS)
                    dve.reciprocal(row_inv[:, :].unsqueeze(2), o_heads[:, :, HD:HV]).then_inc(s["inv_done"], 1)
                if live(known, -2):
                    dve.wait_ge(s["route_step"], (i - 2) * ROUTE_LINKS + 6)
                    link(tt(v3(picked[:, :], TOPK), v3(hot, TOPK),
                            score[:, :].unsqueeze(1).to_broadcast([P, TOPK, EXPERTS]), ALU.mult), until=False)
                if live(known, 0):
                    dve.wait_ge(s["inv_done"], i + 1)
                    tt(v3(attn[:, :], HEADS), o_heads[:, :, 0:HD],
                       row_inv[:, :].unsqueeze(2).to_broadcast([P, HEADS, HD]), ALU.mult).then_inc(s["normed"], 1)
                if live(known, -2):
                    dve.wait_ge(s["route_step"], (i - 2) * ROUTE_LINKS + 7)
                    link(dve.tensor_reduce(scores2[:, cols(i - 2, TOPK)], v3(picked[:, :], TOPK),
                                           axis=AXX, op=ALU.add), until=False)
                    need(dve, s["rank_ps"], i - 2)
                    link(tt(mask_sum[:, :], mask_sum[:, :], mask_bf[:, :], ALU.add), until=False)
                if live(known, -2):
                    dve.wait_ge(s["y_ps"], i - 1)
                    x2 = resid[:, cols(i - 2)]
                    tt(x2, x2, h_b[:, 0:DIM], ALU.add).then_inc(s["acc_done"], 1)
                    dve.wait_ge(s["route_step"], (i - 2) * ROUTE_LINKS + 9)
                    link(tt(mask_bf[:, :], hot0, hot1, ALU.add), until=False)
                if known == FIRST:
                    keys(0)
                    dve.wait_ge(s["masked"], 5 + 2 * CHUNKS)
                    values(0, t_b)
                    dve.wait_ge(s["gate_high"], 1)
                    tt(gate_lo[:, :], gate_raw[:, :], gate_hi[:, :].bitcast(F32), ALU.subtract).then_inc(s["gate_low"], 1)
                    dve.wait_ge(s["bias_in"], 16)
                    dve.wait_ge(s["filled"], 13)
                if known == 0:
                    keys(1)
                    values(1, h_b)

            run_phase_a(dve, step)

            link = chain(s["table_step"], 0)
            dve.wait_ge(s["count_ps"], 1)
            link(dve.tensor_copy(counts[:, :], t_b[:, 0:EXPERTS]))
            link(dve.tensor_copy(counts_i[:, :], counts[:, :]))
            link(tt(v3(over[:, :], EXPERTS), counts[:, :].unsqueeze(2).to_broadcast([P, EXPERTS, TILES]),
                    iota_m[:, :].unsqueeze(1).to_broadcast([P, EXPERTS, TILES]), ALU.is_gt))
            link(dve.tensor_reduce(n_tiles[:, :], v3(over[:, :], EXPERTS), axis=AXX, op=ALU.add))
            link(dve.tensor_tensor_scan(end_tile[:, :], ones_e[:, :], n_tiles[:, :], 0.0, ALU.mult, ALU.add))
            link(tt(start_tile[:, :], end_tile[:, :], n_tiles[:, :], ALU.subtract))
            link(tt(v3(passed[:, :], TILES_B), iota_j[:, :].unsqueeze(2).to_broadcast([P, TILES_B, EXPERTS]),
                    end_tile[:, :].unsqueeze(1).to_broadcast([P, TILES_B, EXPERTS]), ALU.is_ge))
            link(dve.tensor_reduce(expert_f[:, :], v3(passed[:, :], TILES_B), axis=AXX, op=ALU.add))
            link(tt(v3(passed_n[:, :], TILES_B), v3(passed[:, :], TILES_B),
                    n_tiles[:, :].unsqueeze(1).to_broadcast([P, TILES_B, EXPERTS]), ALU.mult))
            link(dve.tensor_reduce(before_f[:, :], v3(passed_n[:, :], TILES_B), axis=AXX, op=ALU.add))
            link(tt(row_f[:, :], iota_j[:, :], before_f[:, :], ALU.subtract))
            link(ts(before_f[:, :], expert_f[:, :], float(REGION), None, ALU.mult))
            link(stt(row_f[:, :], row_f[:, :], float(P), before_f[:, :], ALU.mult, ALU.add))
            link(ts(row_i[:, :], row_f[:, :], float(EXPERTS * REGION), None, ALU.min))
            link(ts(expert_i[:, :], expert_f[:, :], float(EXPERTS - 1), None, ALU.min))

            def x_low(j, par):
                dve.wait_ge(s["b_x_high"], j + 1)
                tt(x2_lo[:, cols(par)], q_b[:, 0:DIM], x2_hi[:, cols(par)].bitcast(F32),
                   ALU.subtract).then_inc(s["b_x_low"], 1)
                a = par * ROW + (ID_EVEN, SCORE)[par]
                dve.tensor_copy(meta[:, cols(par, 2)].bitcast(I32),
                                list_rows[:, a:a + 2].bitcast(I32)).then_inc(s["b_meta"], 1)

            def hidden(j):
                dve.wait_ge(s["b_silu"], j + 1)
                tt(hid[:, :], act_s[:, :], h_b[:, DIM:2 * DIM], ALU.mult).then_inc(s["b_hid"], 1)

            def step_b(j, par, known):
                dve.wait_ge(s["b_meta"], j + 1)
                need(dve, b_out[par], (j - par) * 8)
                dve.tensor_copy(y_meta[:, cols(par, 2)].bitcast(I32),
                                meta[:, cols(par, 2)].bitcast(I32)).then_inc(s["b_y_meta"], 1)
                if known is None or known + 2 < TILES_B:
                    dve.wait_ge(s["b_y_meta"], j + 1)
                    x_low(j + 2, par)
                dve.wait_ge(s["b_h_high"], j + 1)
                tt(h_lo[:, :], t_b[:, 0:DIM], h_hi[:, :].bitcast(F32), ALU.subtract).then_inc(s["b_h_low"], 1)
                if known is None or known + 1 < TILES_B:
                    hidden(j + 1)

            x_low(0, 0)
            x_low(1, 1)
            hidden(0)

            run_phase_b(dve, step_b)

            with dve.Fori(0, TILES // SUM_BUFS) as turn:
                for n in range(SUM_BUFS):
                    t = turn * SUM_BUFS + n
                    acc, rows = resid[:, cols(t)], sum_rows[:, cols(n, TOPK * DIM)]
                    dve.wait_ge(c_in[n], turn * 16 + 16)
                    tt(acc, acc, rows[:, 0:DIM], ALU.add).then_inc(s["c_first"], 1)
                    dve.wait_ge(s["c_first"], t + 1)
                    tt(acc, acc, rows[:, DIM:], ALU.add).then_inc(s["c_sum"], 1)

        @block.tensor
        def _(pe):
            mm = pe.matmul

            def product(to, stationary, moving, start=True, stop=True):
                (ah, al), (bh, bl) = stationary, moving
                mm(to, ah, bl, start=start, stop=False)
                mm(to, al, bh, start=False, stop=False)
                return mm(to, ah, bh, start=False, stop=stop)

            def transposed(to, rows):
                for kt in range(KT):
                    last = pe.transpose(to[:, cols(kt, P)], rows[:, cols(kt, P)], ident[:, :])
                return last

            pe.wait_ge(s["ctx_in"], 16)
            pe.wait_ge(s["wk_in"], 16)
            for half in range(2):
                for kt in range(KT):
                    first_keys = (ctx_t[:, cols(kt, BATCH * 3 * KEYS)]
                                  .rearrange("p (b r) -> p b r", b=BATCH)[:, :, 0:KEYS])
                    last = mm(v3(h_b[:, cols(half, BATCH * KEYS)], BATCH),
                              wk[:, kt * DIM + half * P:kt * DIM + (half + 1) * P], first_keys,
                              start=kt == 0, stop=kt == KT - 1)
            last.then_inc(s["k_ps"], 1)

            def values(b, to):
                for c in range(CHUNKS):
                    for kt in range(KT):
                        a = (kt * BATCH + b) * 3 * KEYS + P * c % KEYS
                        w = kt * DIM + head_base(c) * HD
                        last = mm(to[:, cols(c, VHEADS * HD)], ctx_t[:, a:a + P],
                                  wv[:, w:w + VHEADS * HD], start=kt == 0, stop=kt == KT - 1)
                last.then_inc(s["v_ps"], 1)

            def step(i, par, known, batch):
                if live(known, -3):
                    pe.wait_ge(s["route_step"], (i - 2) * ROUTE_LINKS)
                    mm(t_b[:, 0:EXPERTS], upper[:, :], mask_bf[:, :], start=True, stop=False)
                    mm(t_b[:, 0:EXPERTS], ones[:, :], mask_sum[:, :], start=False, stop=True).then_inc(s["rank_ps"], 1)
                if live(known, 0):
                    if known == 0:
                        pe.wait_ge(s["k_masked"], 4)
                    if known is None and batch == 1:
                        pe.wait_ge(s["k_masked"], 8)
                    pe.wait_ge(s["q_low"], i + 1)
                    need(pe, s["pt_out"], 3 * i)
                    for half in range(2):
                        for r in range(2):
                            rows = slice(64 * r, 64 * r + 64)
                            q = [t[rows, cols(half, P)] for t in (q_hi, q_lo)]
                            k = [t[rows, cols(batch * 2 + half, BANK_COLS)] for t in (k_hi, k_lo)]
                            last = product(bank[2 * half + r][:, 0:BANK_COLS], q, k)
                    last.then_inc(s["s_ps"], 1)
                if live(known, 1):
                    if known == -1:
                        pe.wait_ge(s["masked"], 1)
                    pe.wait_ge(s["xn1"], i + 2)
                    need(pe, s["ot_out"], i)
                    transposed(q_b, xn).then_inc(s["t1_ps"], 1)
                if live(known, -1):
                    if known == 1:
                        pe.wait_ge(s["wo_in"], 16)
                    pe.wait_ge(s["ot_out"], i)
                    for kt in range(KT):
                        last = mm(o_b[:, 0:DIM], attn_t[:, cols(kt, P)], wo[:, cols(kt)],
                                  start=kt == 0, stop=kt == KT - 1)
                    last.then_inc(s["o_ps"], 1)
                if live(known, -2):
                    pe.wait_ge(s["xn2_done"], i - 1)
                    need(pe, s["rank_read"], i - 2)
                    transposed(t_b, xn2[:, cols(par, DIM + 1)]).then_inc(s["t2_ps"], 1)
                if live(known, 1):
                    if known == -1:
                        pe.wait_ge(s["wq_in"], 16)
                    pe.wait_ge(s["t1_out"], i + 2)
                    for half in range(2):
                        for kt in range(KT):
                            last = mm(q_b[:, cols(half, P)], wq[:, kt * DIM + half * P:kt * DIM + (half + 1) * P],
                                      xn_t[:, cols(kt, P)], start=kt == 0, stop=kt == KT - 1)
                    last.then_inc(s["q_ps"], 1)
                if live(known, -2):
                    if known == 2:
                        pe.wait_ge(s["shared_lo"], 1)
                        pe.wait_ge(s["gate_low"], 1)
                    pe.wait_ge(s["x2_low"], i - 1)
                    need(pe, s["acc_done"], i - 2)
                    for kt in range(KT):
                        w = EXPERTS * EW + kt * UP
                        last = product(h_b, [t[:, cols(kt, P)] for t in (x2_hi, x2_lo)],
                                       [t[:, w:w + UP] for t in (w_hi, w_lo)],
                                       start=kt == 0, stop=kt == KT - 1)
                    last.then_inc(s["h_ps"], 1)
                    for kt in range(KT):
                        last = product(t_b[:, 0:EXPERTS], [t[:, cols(kt, P)] for t in (x2_hi, x2_lo)],
                                       [t[:, cols(kt, EXPERTS)] for t in (gate_hi, gate_lo)],
                                       start=kt == 0, stop=kt == KT - 1)
                    last.then_inc(s["gate_ps"], 1)
                if live(known, 0):
                    if known == 0:
                        pe.wait_ge(s["filled"], 13)
                    for c in range(CHUNKS):
                        if c in (0, 4):
                            pe.wait_ge(s["exped"], 2 * i + 1 + c // 4)
                        last = pe.transpose(bank[c // 4][:, cols(c % 4, P)], probs[:, cols(c, P)], ident[:, :])
                        if c % 4 == 3 or c == CHUNKS - 1:
                            last.then_inc(s["pt_ps"], 1)
                if live(known, -2):
                    pe.wait_ge(s["hid_done"], i - 1)
                    pe.wait_ge(s["tanh_g"], i - 1)
                    transposed(t_b, hid).then_inc(s["ht_ps"], 1)
                if live(known, 0):
                    if known == 0:
                        pe.wait_ge(s["v_done"], 2)
                    if known is None and batch == 1:
                        pe.wait_ge(s["v_done"], 4)
                    need(pe, s["x1_done"], i)
                    for c in range(CHUNKS):
                        if c % 4 == 0:
                            pe.wait_ge(s["pt_out"], 3 * i + c // 4 + 1)
                        last = mm(o_b[:, head_base(c) * HV:(head_base(c) + VHEADS) * HV],
                                  probs_t[:, cols(c, P)], vals[:, cols(batch * CHUNKS + c, VHEADS * HV)],
                                  start=c == 0, stop=c == CHUNKS - 1, skip_group_check=True)
                    last.then_inc(s["pv_ps"], 1)
                if live(known, -2):
                    pe.wait_ge(s["h_low"], i - 1)
                    for kt in range(KT):
                        w = EXPERTS * EW + KT * UP + kt * DIM
                        last = product(h_b[:, 0:DIM], [t[:, cols(kt, P)] for t in (h_hi, h_lo)],
                                       [t[:, w:w + DIM] for t in (w_hi, w_lo)],
                                       start=kt == 0, stop=kt == KT - 1)
                    last.then_inc(s["y_ps"], 1)
                if live(known, 0):
                    pe.wait_ge(s["normed"], i + 1)
                    pe.wait_ge(s["q_low"], min(i + 2, TILES) if known is not None else i + 2)
                    transposed(q_b, attn).then_inc(s["ot_ps"], 1)
                if known == FIRST:
                    pe.wait_ge(s["wv_in"], 16)
                    values(0, t_b)
                if known == 0:
                    pe.wait_ge(s["k_out"], 1)
                    values(1, h_b)

            run_phase_a(pe, step)

            pe.wait_ge(s["rank_read"], TILES)
            mm(t_b[:, 0:EXPERTS], ones[:, :], mask_sum[:, :], start=True, stop=False)
            mm(t_b[:, 0:EXPERTS], ones[:, :], mask_bf[:, :], start=False, stop=True).then_inc(s["count_ps"], 1)
            pe.wait_ge(s["split_lo"], SPLIT_STEPS)
            pe.wait_ge(s["table_step"], TABLE_TILES)

            def rows_transposed(j, par):
                pe.wait_ge(b_in[par], (j - par) * 8 + 16)
                need(pe, s["b_x_low"], j)
                transposed(q_b, list_rows[:, cols(par, ROW)]).then_inc(s["b_t_ps"], 1)

            def expert_of(j):
                return pe.value_load(expert_i[0:1, bass.ds(j, 1)], min_val=0, max_val=EXPERTS - 1)

            def gate_up(j, par, expert):
                pe.wait_ge(s["b_x_low"], j + 1)
                for kt in range(KT):
                    last = product(h_b, [t[:, par * DIM + kt * P:par * DIM + (kt + 1) * P] for t in (x2_hi, x2_lo)],
                                   [t[:, bass.ds(expert * EW + kt * UP, UP)] for t in (w_hi, w_lo)],
                                   start=kt == 0, stop=kt == KT - 1)
                last.then_inc(s["b_h_ps"], 1)

            def step_b(j, par, known):
                if known is None or known + 2 < TILES_B:
                    rows_transposed(j + 2, par)
                pe.wait_ge(s["b_hid"], j + 1)
                transposed(t_b, hid).then_inc(s["b_ht_ps"], 1)
                if known is None or known + 1 < TILES_B:
                    gate_up(j + 1, 1 - par, expert_of(j + 1))
                expert = expert_of(j)
                pe.wait_ge(s["b_h_low"], j + 1)
                need(pe, s["b_y"], j)
                for kt in range(KT):
                    last = product(o_b[:, 0:DIM], [t[:, cols(kt, P)] for t in (h_hi, h_lo)],
                                   [t[:, bass.ds(expert * EW + KT * UP + kt * DIM, DIM)] for t in (w_hi, w_lo)],
                                   start=kt == 0, stop=kt == KT - 1)
                last.then_inc(s["b_y_ps"], 1)

            rows_transposed(0, 0)
            rows_transposed(1, 1)
            gate_up(0, 0, expert_of(0))
            run_phase_b(pe, step_b)


_OUT = ((BATCH, SEQ, DIM), "float32")


def _partition_first(w_t):
    n = w_t.shape[-1]
    return np.ascontiguousarray(w_t.reshape(KT, P, n).transpose(1, 0, 2).reshape(P, KT * n))


def kernel(**inputs):
    import concourse.bacc as bacc
    from concourse.bass_utils import run_bass_kernel_spmd

    a = {k.removeprefix("L0_"): np.asarray(v) for k, v in inputs.items()}
    x = np.ascontiguousarray(a["x"].reshape(TOKENS, DIM))
    ctx = np.tile(a["ctx_1024"].transpose(2, 0, 1), (1, 1, 3)).reshape(DIM, BATCH * 3 * KEYS)

    def expert(w1, w3, w2):
        up = _partition_first(np.concatenate([w1.T, w3.T], axis=1))
        return np.concatenate([up, _partition_first(w2.T)], axis=1)

    experts = [expert(a["ffn_w1"][e], a["ffn_w3"][e], a["ffn_w2"][e]) for e in range(EXPERTS)]
    shared = expert(a["ffn_sw1"], a["ffn_sw3"], a["ffn_sw2"])
    arrays = {
        "in_x": x,
        "in_ctx": _partition_first(ctx),
        "in_wq": _partition_first(a["xattn_w_q"].T),
        "in_wk": _partition_first(a["xattn_w_k"].T),
        "in_wv": _partition_first(a["xattn_w_v"].T),
        "in_wo": _partition_first(a["xattn_w_o"].T),
        "in_gate": _partition_first(a["ffn_gate_w"].T),
        "in_bias": np.ascontiguousarray(a["ffn_expert_bias"]),
        "in_ffn": np.ascontiguousarray(np.concatenate(experts + [shared], axis=1)),
    }
    nc = bacc.Bacc("TRN2", target_bir_lowering=False, num_devices=1)
    args = [nc.dram_tensor(n, v.shape, mybir.dt.from_np(v.dtype), kind="ExternalInput").ap()
            for n, v in arrays.items()]
    out = nc.dram_tensor("out_x", (TOKENS, DIM), mybir.dt.from_np(np.dtype(_OUT[1])), kind="ExternalOutput").ap()
    layer_kernel(nc, *args, out)
    r = run_bass_kernel_spmd(nc, [arrays], core_ids=[0])
    return r.results[0]["out_x"].reshape(_OUT[0])
```

```python
import numpy as np
import concourse.bass as bass
from concourse import mybir

F32 = mybir.dt.float32
F32R = mybir.dt.float32r
BF16 = mybir.dt.bfloat16
I32 = mybir.dt.int32
U32 = mybir.dt.uint32
ALU = mybir.AluOpType
ACT = mybir.ActivationFunctionType
AXX = mybir.AxisListType.X

P = 128
BATCH, SEQ, DIM = 2, 1024, 256
KEYS, HEADS = 77, 16
HD = DIM // HEADS
TOKENS = BATCH * SEQ
TILES = TOKENS // P
TILES_PER_BATCH = SEQ // P
KT = DIM // P
EXPERTS, TOPK = 8, 2
EPS = 1e-5
BANK = 512
HEADS_PER_BANK = 4
BANK_COLS = HEADS_PER_BANK * KEYS
HALF_COLS = HEADS * KEYS // 2
CHUNKS = -(-HEADS * KEYS // P)
PCOLS = CHUNKS * P
VHEADS = 3
VN = CHUNKS * VHEADS
HV = HD + 1
UP = 2 * DIM
EW = KT * UP + KT * DIM
PAD_TILES = 4
REGION = TOKENS + PAD_TILES * P
ROW = DIM + 3
ID_EVEN, SCORE, ID_ODD = DIM, DIM + 1, DIM + 2
RESULTS = TOPK * TOKENS
TILES_B = TOPK * TOKENS // P + EXPERTS - 1
SPLIT_STEPS = 12
SPLIT = EXPERTS * EW // SPLIT_STEPS
SUM_GROUPS = [(t, 2) for t in range(0, 14, 2)] + [(14, 1), (15, 1)]
BUSY_PRODUCTS = 72
LIST_BUFS = 4

FIRST, LAST = -2, TILES
TILE_A, TILE_B = TILES - 2, TILES - 1
ROUTE_LINKS, ROUTE_SCORES = 10, 8
LAST_ROUTE_MASK = 8
TABLE_TILES = 13


def head_base(c):
    return min(P * c // KEYS, HEADS - VHEADS)


def need(eng, semaphore, value):
    if not isinstance(value, int) or value > 0:
        eng.wait_ge(semaphore, value)


def live(known, shift):
    return known is None or 0 <= known + shift < TILES


def splitting(known):
    return known is None or 2 <= known < 2 + SPLIT_STEPS


def run_phase_a(eng, step):
    for i in range(FIRST, 4):
        step(i, i % 2, i, 0)
    for batch, (lo, hi) in enumerate(((4, TILES_PER_BATCH), (TILES_PER_BATCH, TILES - 2))):
        with eng.Fori(lo // 2, hi // 2) as turn:
            for par in range(2):
                step(turn * 2 + par, par, None, batch)
    for i in range(TILES - 2, LAST):
        step(i, i % 2, i, 1)


def run_phase_b(eng, step):
    for j in range(LIST_BUFS):
        step(j, j, j)
    with eng.Fori(1, (TILES_B - 3) // LIST_BUFS) as turn:
        for buf in range(LIST_BUFS):
            step(turn * LIST_BUFS + buf, buf, None)
    for j in range(TILES_B - 3, TILES_B):
        step(j, j % LIST_BUFS, j)


def cols(n, width=DIM):
    return bass.ds(n * width, width)


def v3(t, a):
    return t.rearrange("p (a b) -> p a b", a=a)


def layer_kernel(nc, x, ctxt, wqt, wkt, wvt, wot, gatet, bias, wffn, out):
    def sb(name, n, dt=F32):
        return nc.alloc_sbuf_tensor(name, [P, n], dt)

    lists = nc.dram_tensor("lists", [EXPERTS * REGION + P, ROW], F32, kind="Internal").ap()
    value_rows = nc.dram_tensor("value_rows", [BATCH, HEADS * KEYS, HD], F32, kind="Internal").ap()
    results = nc.dram_tensor("results", [RESULTS + 2 * P, DIM], F32, kind="Internal").ap()

    resid = sb("resid", TILES * DIM)
    wq, wk, wv, wo = (sb(n, KT * DIM) for n in ("wq", "wk", "wv", "wo"))
    gate_raw = sb("gate_raw", KT * EXPERTS)
    gate_hi = sb("gate_hi", KT * EXPERTS, F32R)
    gate_lo = sb("gate_lo", KT * EXPERTS, F32R)
    bias_b = sb("bias_b", EXPERTS)
    ctx_t = sb("ctx_t", KT * BATCH * KEYS)
    w_stage = sb("w_stage", 2 * SPLIT)
    w_hi = sb("w_hi", (EXPERTS + 1) * EW, F32R)
    w_lo = sb("w_lo", (EXPERTS + 1) * EW, F32R)
    k_raw = sb("k_raw", 2 * BATCH * KEYS)
    k_raw_hi = sb("k_raw_hi", 2 * BATCH * KEYS, F32R)
    k_raw_lo = sb("k_raw_lo", 2 * BATCH * KEYS, F32R)
    k_hi = sb("k_hi", BATCH * 2 * BANK_COLS, F32R)
    k_lo = sb("k_lo", BATCH * 2 * BANK_COLS, F32R)
    vals = sb("vals", BATCH * VN * HV)
    ident = sb("ident", P)
    head_of, head_mask = sb("head_of", 2 * HEADS_PER_BANK), sb("head_mask", HEADS_PER_BANK)
    val_mask = sb("val_mask", VN)
    upper = sb("upper", P, BF16)
    ones = sb("ones", P, BF16)
    minus_half, silu_table = sb("minus_half", 1), sb("silu_table", 1)
    iota_e = sb("iota_e", EXPERTS)
    iota_m = sb("iota_m", TILES)
    iota_j = sb("iota_j", TILES_B)
    ones_e = sb("ones_e", EXPERTS)
    pad_rows = sb("pad_rows", ROW)
    ids = sb("ids", TILES * TOPK, I32)
    stats1, mv1, ve1, rstd1 = sb("stats1", 6), sb("mv1", 2), sb("ve1", 1), sb("rstd1", 1)
    stats2, mv2, ve2, rstd2 = sb("stats2", 6), sb("mv2", 2), sb("ve2", 1), sb("rstd2", 1)
    xn, xn_t = sb("xn", DIM), sb("xn_t", DIM)
    q_hi, q_lo = sb("q_hi", DIM, F32R), sb("q_lo", DIM, F32R)
    row_max, row_inv = sb("row_max", HEADS), sb("row_inv", HEADS)
    probs, probs_t = sb("probs", PCOLS), sb("probs_t", PCOLS)
    sum_tiles = w_hi[:, 0:TILES * TOPK * DIM].bitcast(F32).rearrange("p (t w) -> p t w", t=TILES)
    attn, attn_t = sb("attn", DIM), sb("attn_t", DIM)
    xn2 = sb("xn2", 2 * (DIM + 1))
    x2_hi, x2_lo = sb("x2_hi", 2 * DIM, F32R), sb("x2_lo", 2 * DIM, F32R)
    act_s, silu_s, hid = sb("act_s", DIM), sb("silu_s", DIM), sb("hid", 2 * DIM)
    h_hi, h_lo = sb("h_hi", DIM, F32R), sb("h_lo", DIM, F32R)
    th8, score, ranked, top8 = (sb(n, EXPERTS) for n in ("th8", "score", "ranked", "top8"))
    top8_i = sb("top8_i", EXPERTS, U32)
    chosen_f = sb("chosen_f", TOPK)
    picked = sb("picked", TOPK * EXPERTS)
    mask_bf, mask_sum = sb("mask_bf", EXPERTS, BF16), sb("mask_sum", EXPERTS, BF16)
    onehot, picked_r = sb("onehot", 2 * TOPK * EXPERTS), sb("picked_r", TOPK * EXPERTS)
    scores2, ranks2 = sb("scores2", TILES * TOPK), sb("ranks2", TOPK)
    dest_f, dest = sb("dest_f", TOPK), sb("dest", 2 * TOPK, I32)
    row_space = sb("row_space", LIST_BUFS * ROW)
    scaled = list_rows = row_space
    v_raw = row_space[0:KEYS, 0:BATCH * DIM]
    v_rows = row_space[:, BATCH * DIM:BATCH * DIM + BATCH * CHUNKS * HD]
    counts, counts_i = sb("counts", EXPERTS), sb("counts_i", EXPERTS, I32)
    over = sb("over", EXPERTS * TILES)
    n_tiles, end_tile = sb("n_tiles", EXPERTS), sb("end_tile", EXPERTS)
    passed, passed_n = sb("passed", TILES_B * EXPERTS), sb("passed_n", TILES_B * EXPERTS)
    expert_f, before_f, row_f = (sb(n, TILES_B) for n in ("expert_f", "before_f", "row_f"))
    column_i, row_i = sb("column_i", TILES_B, I32), sb("row_i", TILES_B, I32)
    y_rows = sb("y_rows", 2 * DIM)
    meta = sb("meta", 2 * TILES_B)

    psum = nc.alloc_psum_tensor("psum", [P, 8 * BANK], F32)
    bank = [psum[:, n * BANK:(n + 1) * BANK] for n in range(8)]
    o_b, q_b, t_b, h_b = bank[4:8]
    hidden_b = (h_b, bank[0])
    score_view = (psum[:, 0:4 * BANK].rearrange("p (g c) -> p g c", g=4)[:, :, 0:BANK_COLS]
                  .rearrange("p g (h k) -> p g h k", k=KEYS))

    s = {name: nc.alloc_semaphore(name) for name in (
        "x0_in x1_in x2_in ctx_in wk_in wq_in wv_in wo_in gate_in bias_in shared_in split_in0 split_in1 "
        "early_counts table_in filled masked pads_done k_ps k_out k_low k_masked "
        "v_ps v_out v_stored v_in0 v_in1 v_done gate_high gate_low "
        "shared_hi shared_lo split_hi split_lo "
        "ln1_step pow1 xn1 t1_ps t1_out q_ps q_high q_low s_ps maxed subbed exped pt_ps pt_out "
        "pv_ps inv_done normed ot_ps ot_out o_ps x1_done ln2_step pow2 xn2_done "
        "t2_ps x2_high x2_low h_ps tanh_h silu_done hid_done gate_ps tanh_g route_step scaled_done "
        "rank_ps rank_read scat0 scat1 ht_ps h_high h_low y_ps acc_done table_step dest_step pad_out "
        "b_in0 b_in1 b_in2 b_in3 b_t_ps b_x_high b_x_low b_h_ps b_silu b_hid b_ht_ps b_h_high b_h_low b_y_ps "
        "b_y b_meta b_out0 b_out1 c_in0 c_in1 c_in2 c_in3 c_in4 c_in5 c_in6 c_in7 c_in8 "
        "c_first c_sum c_out").split()}
    split_in, scat = [s["split_in0"], s["split_in1"]], [s["scat0"], s["scat1"]]
    b_in, b_out = [s[f"b_in{n}"] for n in range(LIST_BUFS)], [s["b_out0"], s["b_out1"]]
    c_in = [s[f"c_in{n}"] for n in range(len(SUM_GROUPS))]

    with nc.Block() as block:

        @block.sync
        def _(sp):
            x_tiles = x.rearrange("(t p) d -> p t d", p=P)
            resid_tiles = resid[:, :].rearrange("p (t d) -> p t d", d=DIM)
            sp.dma_start(wk[:, :], wkt).then_inc(s["wk_in"], 16)
            sp.dma_start(resid_tiles[:, 0:2, :], x_tiles[:, 0:2, :]).then_inc(s["x0_in"], 16)
            sp.dma_start(wv[:, :], wvt).then_inc(s["wv_in"], 16)
            sp.dma_start(wo[:, :], wot).then_inc(s["wo_in"], 16)
            sp.dma_start(resid_tiles[:, 2:9, :], x_tiles[:, 2:9, :]).then_inc(s["x1_in"], 16)

            sp.dma_start(w_stage[:, 0:EW], wffn[:, EXPERTS * EW:(EXPERTS + 1) * EW]).then_inc(s["shared_in"], 16)
            sp.wait_ge(s["v_stored"], 16)
            sp.wait_ge(s["filled"], 14)
            full, rest = divmod(HEADS * KEYS, P)
            for b in range(BATCH):
                to = v3(v_rows[:, cols(b, CHUNKS * HD)], CHUNKS)
                sp.dma_start(to[:, 0:full, :], value_rows[b, 0:full * P, :]
                             .rearrange("(c p) d -> p c d", p=P)).then_inc(s[f"v_in{b}"], 16)
                sp.dma_start(to[0:rest, full, :], value_rows[b, full * P:, :]).then_inc(s[f"v_in{b}"], 16)
            sp.dma_start(resid_tiles[:, 9:, :], x_tiles[:, 9:, :]).then_inc(s["x2_in"], 16)
            sp.wait_ge(s["shared_lo"], 1)
            for n in range(2):
                sp.dma_start(w_stage[:, n * SPLIT:(n + 1) * SPLIT],
                             wffn[:, n * SPLIT:(n + 1) * SPLIT]).then_inc(split_in[n], 16)
            with sp.Fori(0, SPLIT_STEPS // 2 - 1) as turn:
                for par in range(2):
                    sp.wait_ge(s["split_lo"], turn * 2 + par + 1)
                    sp.dma_start(w_stage[:, cols(par, SPLIT)],
                                 wffn[:, cols(turn * 2 + par + 2, SPLIT)]).then_inc(split_in[par], 16)

            sp.wait_ge(s["early_counts"], 1)
            sp.wait_ge(s["pads_done"], 5)
            zeros = pad_rows[:, :].unsqueeze(1).to_broadcast([P, PAD_TILES, ROW])
            for e in range(EXPERTS):
                n_rows = sp.value_load(counts_i[0:1, e:e + 1], min_val=0, max_val=TOKENS)
                sp.dma_start(lists[bass.ds(n_rows + e * REGION, PAD_TILES * P), :]
                             .rearrange("(a p) d -> p a d", p=P), zeros).then_inc(s["pad_out"], 16)
            sp.dma_start(lists[EXPERTS * REGION:, :], pad_rows[:, :]).then_inc(s["pad_out"], 16)
            sp.wait_ge(s["table_step"], TABLE_TILES)

            def load(j, buf, known):
                row = sp.value_load(row_i[0:1, bass.ds(j, 1)], min_val=0, max_val=EXPERTS * REGION)
                if known == 0:
                    sp.wait_ge(s["pad_out"], 16 * (EXPERTS + 1))
                    for par in range(2):
                        sp.wait_ge(scat[par], 16 * TOPK * (TILES // 2))
                need(sp, s["b_t_ps"], j - LIST_BUFS + 1)
                need(sp, s["b_meta"], j - LIST_BUFS + 1)
                sp.dma_start(list_rows[:, cols(buf, ROW)], lists[bass.ds(row, P), :]).then_inc(b_in[buf], 16)

            run_phase_b(sp, load)

            for par in range(2):
                sp.wait_ge(b_out[par], 16 * ((TILES_B + 1 - par) // 2))
            token_rows = results[0:RESULTS, :].rearrange("(t k) d -> t (k d)", k=TOPK)
            token_tiles = token_rows.rearrange("(t p) w -> p t w", p=P)
            for n, (t, tiles) in enumerate(SUM_GROUPS):
                sp.dma_start(sum_tiles[:, t:t + tiles, :], token_tiles[:, t:t + tiles, :]).then_inc(c_in[n], 16)

        @block.gpsimd
        def _(pool):
            fills = ((ident, 0.0), (head_of, 1.0), (val_mask, 1.0), (upper, 1.0), (ones, 1.0),
                     (minus_half, -0.5), (mask_sum, 0.0), (mask_bf, 0.0), (ones_e, 1.0))
            once = ((pad_rows, 0, ROW, 0.0), (xn2, DIM, DIM + 1, 1.0), (xn2, 2 * DIM + 1, 2 * DIM + 2, 1.0))
            for t, value in fills:
                pool.memset(t[:, :], value).then_inc(s["filled"], 1)
            pool.memset(probs[:, HEADS * KEYS:PCOLS], 0.0).then_inc(s["filled"], 1)
            pool.memset(v_rows, 0.0).then_inc(s["filled"], 1)
            for t, pitch, n in ((iota_e, 1, EXPERTS), (iota_m, P, TILES), (iota_j, 1, TILES_B)):
                pool.iota(t[:, :], pattern=[[pitch, n]], base=0, channel_multiplier=0,
                          allow_small_or_imprecise_dtypes=True).then_inc(s["filled"], 1)
            pool.wait_ge(s["filled"], 14)

            def cut(t, op, fill, base, pattern, per_partition):
                pool.affine_select(out=t, in_=t, compare_op=op, fill=fill, base=base, pattern=[pattern],
                                   channel_multiplier=per_partition).then_inc(s["masked"], 1)

            cut(ident[:, :], ALU.not_equal, 1.0, 0, [-1, P], 1)
            cut(head_of[:, :], ALU.is_ge, 0.0, 0, [-HD, 2 * HEADS_PER_BANK], 1)
            pool.wait_ge(s["masked"], 2)
            cut(head_of[:, :], ALU.is_ge, 0.0, HD - 1, [HD, 2 * HEADS_PER_BANK], -1)
            pool.wait_ge(s["masked"], 3)
            pool.tensor_tensor(head_mask[:, :], head_of[:, 0:HEADS_PER_BANK], head_of[:, HEADS_PER_BANK:],
                               ALU.add).then_inc(s["masked"], 1)
            for c in range(CHUNKS):
                cut(val_mask[:, cols(c, VHEADS)], ALU.is_ge, 0.0, P * c - KEYS * head_base(c),
                    [-KEYS, VHEADS], 1)
            pool.wait_ge(s["masked"], 4 + CHUNKS)
            for c in range(CHUNKS):
                cut(val_mask[:, cols(c, VHEADS)], ALU.is_ge, 0.0, KEYS * head_base(c) + KEYS - 1 - P * c,
                    [KEYS, VHEADS], -1)
            cut(upper[:, :], ALU.is_ge, 0.0, -1, [1, P], -1)
            for t, a, b, value in once:
                pool.memset(t[:, a:b], value).then_inc(s["pads_done"], 1)
            pool.wait_ge(s["pads_done"], 3)
            for a, extra in ((ID_EVEN, 0), (ID_ODD, P)):
                pool.iota(pad_rows[:, a:a + 1].bitcast(I32), pattern=[[0, 1]], base=RESULTS + extra,
                          channel_multiplier=1).then_inc(s["pads_done"], 1)
            pool.iota(ids[:, :], pattern=[[P * TOPK, TILES], [1, TOPK]], base=0,
                      channel_multiplier=TOPK).then_inc(s["pads_done"], 1)

            def scatter(par):
                for k in range(TOPK):
                    n = par * TOPK + k
                    pool.indirect_dma_start(
                        lists, bass.IndirectOffsetOnAxis(ap=dest[:, n:n + 1], axis=0),
                        scaled[:, cols(n, ROW)], None).then_inc(scat[par], 16)

            def scale_rows(t, par, links):
                pool.wait_ge(s["route_step"], t * ROUTE_LINKS + links)
                need(pool, scat[par], (t - par) * 8 * TOPK)
                for k in range(TOPK):
                    n = par * TOPK + k
                    a = n * ROW
                    score_k = scores2[:, cols(t * TOPK + k, 1)]
                    xs = xn2[:, cols(par, DIM + 1)]
                    pool.tensor_tensor(scaled[:, a:a + DIM], xs[:, 0:DIM],
                                       score_k.to_broadcast([P, DIM]), ALU.mult).then_inc(s["scaled_done"], 1)
                    pool.tensor_tensor(scaled[:, a + SCORE:a + SCORE + 1], xs[:, DIM:DIM + 1],
                                       score_k, ALU.mult).then_inc(s["scaled_done"], 1)
                    pool.tensor_copy(scaled[:, a + ID_EVEN:a + ID_ODD + 1:2].bitcast(I32),
                                     ids[:, cols(t * TOPK + k, 1)].to_broadcast([P, 2])
                                     ).then_inc(s["scaled_done"], 1)

            def step(i, par, known, _):
                if live(known, -1):
                    pool.wait_ge(s["ln2_step"], 3 * i)
                    pool.tensor_tensor(rstd2[:, :], ve2[:, :], minus_half[:, :], ALU.pow).then_inc(s["pow2"], 1)
                if live(known, -3):
                    pool.wait_ge(s["scaled_done"], 3 * TOPK * (i - 2))
                    pool.wait_ge(s["dest_step"], 3 * (i - 2))
                if live(known, 2):
                    pool.wait_ge(s["ln1_step"], 3 * (i + 3))
                    pool.tensor_tensor(rstd1[:, :], ve1[:, :], minus_half[:, :], ALU.pow).then_inc(s["pow1"], 1)
                if live(known, -3):
                    scatter(1 - par)
                if known == -1:
                    pool.wait_ge(s["shared_hi"], 1)
                    pool.tensor_tensor(w_lo[:, cols(EXPERTS, EW)], w_stage[:, 0:EW],
                                       w_hi[:, cols(EXPERTS, EW)].bitcast(F32),
                                       ALU.subtract).then_inc(s["shared_lo"], 1)
                if splitting(known):
                    pool.wait_ge(s["split_hi"], i - 1)
                    pool.tensor_tensor(w_lo[:, cols(i - 2, SPLIT)], w_stage[:, cols(par, SPLIT)],
                                       w_hi[:, cols(i - 2, SPLIT)].bitcast(F32),
                                       ALU.subtract).then_inc(s["split_lo"], 1)
                if live(known, -2):
                    if known == 2:
                        pool.wait_ge(s["pads_done"], 6)
                    scale_rows(i - 2, par, ROUTE_SCORES)

            run_phase_a(pool, step)

            pool.wait_ge(s["ln2_step"], 3 * TILES)
            pool.tensor_tensor(rstd2[:, :], ve2[:, :], minus_half[:, :], ALU.pow).then_inc(s["pow2"], 1)
            for t, links in ((TILE_A, ROUTE_SCORES), (TILE_B, ROUTE_LINKS), (TILES, None)):
                pool.wait_ge(s["scaled_done"], 3 * TOPK * t)
                pool.wait_ge(s["dest_step"], 3 * t)
                if t == TILE_A:
                    pool.wait_ge(s["pad_out"], 16 * (EXPERTS + 1))
                scatter((t - 1) % 2)
                if links:
                    scale_rows(t, t % 2, links)

            for j in range(TILES_B):
                par = j % 2
                pool.wait_ge(s["b_y"], j + 1)
                index = meta[:, 2 * j + par:2 * j + par + 1].bitcast(I32)
                pool.indirect_dma_start(
                    results, bass.IndirectOffsetOnAxis(ap=index, axis=0),
                    y_rows[:, cols(par)], None).then_inc(b_out[par], 16)

        @block.scalar
        def _(act):
            act.dma_start(ctx_t[:, :], ctxt).then_inc(s["ctx_in"], 16)
            act.dma_start(wq[:, :], wqt).then_inc(s["wq_in"], 16)
            act.dma_start(gate_raw[:, :], gatet).then_inc(s["gate_in"], 16)
            act.dma_start(bias_b[:, :], bias.partition_broadcast(P)).then_inc(s["bias_in"], 16)
            act.wait_ge(s["k_ps"], 1)
            act.activation(k_raw[:, :], h_b[:, 0:2 * BATCH * KEYS], ACT.Copy).then_inc(s["k_out"], 1)
            act.wait_ge(s["k_out"], 1)
            act.activation(k_raw_hi[:, :], k_raw[:, :], ACT.Copy).then_inc(s["k_out"], 1)
            act.wait_ge(s["v_ps"], 1)
            act.activation(v_raw, bank[0][0:KEYS, 0:BATCH * DIM], ACT.Copy).then_inc(s["v_out"], 1)
            act.wait_ge(s["v_out"], 1)
            act.dma_start(value_rows.rearrange("b (h k) d -> k b h d", k=KEYS),
                          v_raw.rearrange("k (b h d) -> k b h d", b=BATCH, d=HD)).then_inc(s["v_stored"], 16)
            act.wait_ge(s["gate_in"], 16)
            act.activation(gate_hi[:, :], gate_raw[:, :], ACT.Copy).then_inc(s["gate_high"], 1)

            def exponentials(i, g):
                act.wait_ge(s["subbed"], 2 * i + g + 1)
                part = probs[:, cols(g, HALF_COLS)]
                act.activation(part, part, ACT.Exp, scale=float(HD) ** -0.5).then_inc(s["exped"], 1)

            def step(i, par, known, _):
                if live(known, -1):
                    act.wait_ge(s["ot_ps"], i)
                    act.activation(attn_t[:, :], q_b[:, 0:DIM], ACT.Copy).then_inc(s["ot_out"], 1)
                if live(known, 1):
                    act.wait_ge(s["t1_ps"], i + 2)
                    act.activation(xn_t[:, :], q_b[:, 0:DIM], ACT.Copy).then_inc(s["t1_out"], 1)
                if live(known, -2):
                    act.wait_ge(s["t2_ps"], i - 1)
                    act.activation(x2_hi[:, 0:DIM], t_b[:, 0:DIM], ACT.Copy).then_inc(s["x2_high"], 1)
                if live(known, 1):
                    act.wait_ge(s["q_ps"], i + 2)
                    act.activation(q_hi[:, :], q_b[:, 0:DIM], ACT.Copy).then_inc(s["q_high"], 1)
                if live(known, 0):
                    exponentials(i, 0)
                if live(known, -2):
                    act.wait_ge(s["h_ps"], i - 1)
                    need(act, s["silu_done"], i - 2)
                    act.activation(act_s[:, :], h_b[:, 0:DIM], ACT.Tanh, scale=0.5).then_inc(s["tanh_h"], 1)
                if live(known, 0):
                    exponentials(i, 1)
                if live(known, -2):
                    act.wait_ge(s["gate_ps"], i - 1)
                    act.activation(th8[:, :], t_b[:, 0:EXPERTS], ACT.Tanh, scale=0.5).then_inc(s["tanh_g"], 1)
                if live(known, 0):
                    for g in range(3):
                        act.wait_ge(s["pt_ps"], 3 * i + g + 1)
                        n = min(BANK, PCOLS - BANK * g)
                        act.activation(probs_t[:, BANK * g:BANK * g + n], bank[g][:, 0:n],
                                       ACT.Copy).then_inc(s["pt_out"], 1)
                if live(known, -2):
                    act.wait_ge(s["ht_ps"], i - 1)
                    act.activation(h_hi[:, :], t_b[:, 0:DIM], ACT.Copy).then_inc(s["h_high"], 1)
                if splitting(known):
                    act.wait_ge(split_in[par], (i - par) * 8)
                    act.activation(w_hi[:, cols(i - 2, SPLIT)], w_stage[:, cols(par, SPLIT)],
                                   ACT.Copy).then_inc(s["split_hi"], 1)
                if known == -1:
                    act.wait_ge(s["shared_in"], 16)
                    act.activation(w_hi[:, cols(EXPERTS, EW)], w_stage[:, 0:EW], ACT.Copy).then_inc(s["shared_hi"], 1)

            run_phase_a(act, step)

            def copied(to, source, ready, value, done):
                act.wait_ge(s[ready], value)
                act.activation(to, source, ACT.Copy).then_inc(s[done], 1)

            def tanh(to, source, ready, value, done):
                act.wait_ge(s[ready], value)
                act.activation(to, source, ACT.Tanh, scale=0.5).then_inc(s[done], 1)

            copied(attn_t[:, :], q_b[:, 0:DIM], "ot_ps", TILES, "ot_out")
            copied(x2_hi[:, cols(0)], t_b[:, 0:DIM], "t2_ps", TILES - 1, "x2_high")
            tanh(th8[:, :], t_b[:, 0:EXPERTS], "gate_ps", TILES - 1, "tanh_g")
            tanh(act_s[:, :], h_b[:, 0:DIM], "h_ps", TILES - 1, "tanh_h")
            copied(x2_hi[:, cols(1)], q_b[:, 0:DIM], "t2_ps", TILES, "x2_high")
            act.wait_ge(s["route_step"], TILE_A * ROUTE_LINKS + 1)
            tanh(th8[:, :], t_b[:, 0:EXPERTS], "gate_ps", TILES, "tanh_g")
            act.wait_ge(s["silu_done"], TILES - 1)
            tanh(act_s[:, :], bank[0][:, 0:DIM], "h_ps", TILES, "tanh_h")
            copied(h_hi[:, :], t_b[:, 0:DIM], "ht_ps", TILES - 1, "h_high")
            copied(h_hi[:, :], q_b[:, 0:DIM], "ht_ps", TILES, "h_high")
            act.activation(silu_table[:, :], minus_half[:, :], ACT.Silu).then_inc(s["table_in"], 1)

            def x_high(j, par):
                act.wait_ge(s["b_t_ps"], j + 1)
                act.activation(x2_hi[:, cols(par)], q_b[:, 0:DIM], ACT.Copy).then_inc(s["b_x_high"], 1)

            def silu(j, par):
                act.wait_ge(s["b_h_ps"], j + 1)
                need(act, s["b_hid"], j)
                act.activation(act_s[:, :], hidden_b[par][:, 0:DIM], ACT.Silu).then_inc(s["b_silu"], 1)

            def step_b(j, buf, known):
                par = buf % 2
                act.wait_ge(s["b_ht_ps"], j + 1)
                act.activation(h_hi[:, :], t_b[:, 0:DIM], ACT.Copy).then_inc(s["b_h_high"], 1)
                if known is None or known + 3 < TILES_B:
                    x_high(j + 3, 1 - par)
                if known is None or known + 2 < TILES_B:
                    silu(j + 2, par)
                act.wait_ge(s["b_y_ps"], j + 1)
                act.wait_ge(s["b_meta"], j + 1)
                need(act, b_out[par], (j - par) * 8)
                act.activation(y_rows[:, cols(par)], o_b[:, 0:DIM], ACT.Copy,
                               scale=meta[:, bass.ds(2 * j + 1 - par, 1)]).then_inc(s["b_y"], 1)

            x_high(0, 0)
            x_high(1, 1)
            silu(0, 0)
            x_high(2, 0)
            silu(1, 1)
            run_phase_b(act, step_b)

            out_tiles, resid_tiles = out.rearrange("(t p) d -> p t d", p=P), v3(resid[:, :], TILES)
            for n, (t, tiles) in enumerate(SUM_GROUPS):
                act.wait_ge(s["c_sum"], n + 1)
                act.dma_start(out_tiles[:, t:t + tiles, :], resid_tiles[:, t:t + tiles, :]).then_inc(s["c_out"], 16)
            act.wait_ge(s["c_out"], 16 * len(SUM_GROUPS))

        @block.vector
        def _(dve):
            tt, stt, ts = dve.tensor_tensor, dve.scalar_tensor_tensor, dve.tensor_scalar

            def chain(semaphore, before):
                count = [0]

                def link(ins, until=True):
                    count[0] += 1
                    ins.then_inc(semaphore, 1)
                    if until:
                        dve.wait_ge(semaphore, before + count[0])
                return link

            def values(b):
                dve.wait_ge(s[f"v_in{b}"], 32)
                view = v3(vals[:, cols(b, VN * HV)], VN)
                rows = v3(v_rows[:, cols(b, CHUNKS * HD)], CHUNKS)
                for h in range(VHEADS):
                    tt(view[:, h::VHEADS, 0:HD], rows, val_mask[:, h::VHEADS].unsqueeze(2)
                       .to_broadcast([P, CHUNKS, HD]), ALU.mult).then_inc(s["v_done"], 1)
                dve.tensor_copy(view[:, :, HD:HV], val_mask[:, :].unsqueeze(2)).then_inc(s["v_done"], 1)

            def keys(b):
                for half in range(2):
                    for raw, part in ((k_raw_hi, k_hi), (k_raw_lo, k_lo)):
                        tt(v3(part[:, cols(b * 2 + half, BANK_COLS)], HEADS_PER_BANK),
                           raw[:, cols(half * BATCH + b, KEYS)].bitcast(F32).unsqueeze(1)
                           .to_broadcast([P, HEADS_PER_BANK, KEYS]),
                           head_mask[:, :].unsqueeze(2).to_broadcast([P, HEADS_PER_BANK, KEYS]),
                           ALU.mult).then_inc(s["k_masked"], 1)

            def less_max(g):
                tt(probs[:, cols(g, HALF_COLS)].rearrange("p (b h k) -> p b h k", b=2, k=KEYS),
                   score_view[:, 2 * g:2 * g + 2, :, :],
                   v3(row_max[:, cols(g, HEADS // 2)], 2).unsqueeze(3)
                   .to_broadcast([P, 2, HEADS_PER_BANK, KEYS]), ALU.subtract).then_inc(s["subbed"], 1)

            def step(i, par, known, _):
                if live(known, -3):
                    place = chain(s["dest_step"], (i - 3) * 3)
                    ranks = ranks2[:, :]
                    dve.wait_ge(s["rank_ps"], i - 2)
                    if known == LAST - 1:
                        dve.tensor_copy(counts_i[:, :], t_b[:, EXPERTS:2 * EXPERTS]).then_inc(s["early_counts"], 1)
                    tt(v3(picked_r[:, :], TOPK), v3(onehot[:, cols(1 - par, TOPK * EXPERTS)], TOPK),
                       t_b[:, 0:EXPERTS].unsqueeze(1).to_broadcast([P, TOPK, EXPERTS]),
                       ALU.mult).then_inc(s["rank_read"], 1)
                if live(known, 0):
                    dve.wait_ge(s["s_ps"], i + 1)
                    dve.tensor_reduce(v3(row_max[:, :], 4), score_view, axis=AXX, op=ALU.max).then_inc(s["maxed"], 1)
                if live(known, -3):
                    dve.wait_ge(s["rank_read"], i - 2)
                    place(dve.tensor_reduce(ranks, v3(picked_r[:, :], TOPK), axis=AXX, op=ALU.add), until=False)
                if live(known, -2):
                    dve.wait_ge(s["x2_high"], i - 1)
                    tt(x2_lo[:, 0:DIM], t_b[:, 0:DIM], x2_hi[:, 0:DIM].bitcast(F32),
                       ALU.subtract).then_inc(s["x2_low"], 1)
                if live(known, 0):
                    dve.wait_ge(s["maxed"], i + 1)
                    less_max(0)
                if live(known, -1):
                    dve.wait_ge(s["o_ps"], i)
                    x1 = resid[:, cols(i - 1)]
                    tt(x1, x1, o_b[:, 0:DIM], ALU.add).then_inc(s["x1_done"], 1)
                if live(known, 0):
                    less_max(1)
                if live(known, -1):
                    dve.wait_ge(s["x1_done"], i)
                if live(known, -3):
                    dve.wait_ge(s["dest_step"], (i - 3) * 3 + 1)
                    place(stt(dest_f[:, :], chosen_f[:, :], float(REGION), ranks, ALU.mult, ALU.add), until=False)
                norms = []
                if live(known, -1):
                    norms.append((s["ln2_step"], (i - 1) * 3, stats2, mv2, ve2))
                    dve.bn_stats(stats2[:, :], x1).then_inc(s["ln2_step"], 1)
                if live(known, -2):
                    dve.wait_ge(s["tanh_h"], i - 1)
                    stt(silu_s[:, :], act_s[:, :], 1.0, h_b[:, 0:DIM], ALU.add, ALU.mult).then_inc(s["silu_done"], 1)
                if live(known, -3):
                    dve.wait_ge(s["dest_step"], (i - 3) * 3 + 2)
                    dve.wait_ge(s["scaled_done"], 3 * TOPK * (i - 2))
                    place(dve.tensor_copy(dest[:, cols(1 - par, TOPK)], dest_f[:, :]), until=False)
                if live(known, -2):
                    dve.wait_ge(s["silu_done"], i - 1)
                    stt(hid[:, 0:DIM], silu_s[:, :], 0.5, h_b[:, DIM:2 * DIM], ALU.mult, ALU.mult).then_inc(s["hid_done"], 1)
                if live(known, 2):
                    if known == FIRST:
                        dve.wait_ge(s["x0_in"], 16)
                    if known == 0:
                        dve.wait_ge(s["x1_in"], 16)
                    if known == 3:
                        dve.wait_ge(s["x2_in"], 16)
                    x0 = resid[:, cols(i + 2)]
                    norms.append((s["ln1_step"], (i + 2) * 3, stats1, mv1, ve1))
                    dve.bn_stats(stats1[:, :], x0).then_inc(s["ln1_step"], 1)
                for done, before, st, mv, ve in norms:
                    dve.wait_ge(done, before + 1)
                if live(known, 1):
                    dve.wait_ge(s["q_high"], i + 2)
                    tt(q_lo[:, :], q_b[:, 0:DIM], q_hi[:, :].bitcast(F32), ALU.subtract).then_inc(s["q_low"], 1)
                for done, before, st, mv, ve in norms:
                    dve.bn_aggr(mv[:, :], st[:, :]).then_inc(done, 1)
                for done, before, st, mv, ve in norms:
                    dve.wait_ge(done, before + 2)
                    ts(ve[:, :], mv[:, 1:2], EPS, None, ALU.add).then_inc(done, 1)
                if live(known, -2):
                    link = chain(s["route_step"], (i - 2) * ROUTE_LINKS)
                    hot = onehot[:, cols(par, TOPK * EXPERTS)]
                    hot0, hot1 = hot[:, 0:EXPERTS], hot[:, EXPERTS:]
                    dve.wait_ge(s["tanh_g"], i - 1)
                    link(ts(score[:, :], th8[:, :], 0.5, 0.5, ALU.mult, ALU.add))
                    link(tt(ranked[:, :], score[:, :], bias_b[:, :], ALU.add))
                if live(known, -2):
                    dve.wait_ge(s["h_high"], i - 1)
                    tt(h_lo[:, :], t_b[:, 0:DIM], h_hi[:, :].bitcast(F32), ALU.subtract).then_inc(s["h_low"], 1)
                    link(dve.max(top8[:, :], ranked[:, :]), until=False)
                if live(known, -2):
                    dve.wait_ge(s["route_step"], (i - 2) * ROUTE_LINKS + 3)
                if live(known, -1):
                    dve.wait_ge(s["pow2"], i)
                    need(dve, s["scaled_done"], 3 * TOPK * (i - 2))
                    ts(xn2[:, (1 - par) * (DIM + 1):(1 - par) * (DIM + 1) + DIM], x1, mv2[:, 0:1], rstd2[:, :],
                       ALU.subtract, ALU.mult).then_inc(s["xn2_done"], 1)
                if live(known, -2):
                    link(dve.max_index(top8_i[:, :], top8[:, :], ranked[:, :]), until=False)
                if live(known, 2):
                    dve.wait_ge(s["pow1"], i + 3)
                    need(dve, s["t1_ps"], i + 2)
                    ts(xn[:, :], x0, mv1[:, 0:1], rstd1[:, :], ALU.subtract, ALU.mult).then_inc(s["xn1"], 1)
                if live(known, -2):
                    dve.wait_ge(s["route_step"], (i - 2) * ROUTE_LINKS + 4)
                    link(dve.tensor_copy(chosen_f[:, :], top8_i[:, 0:TOPK]))
                    link(tt(v3(hot, TOPK), iota_e[:, :].unsqueeze(1).to_broadcast([P, TOPK, EXPERTS]),
                            chosen_f[:, :].unsqueeze(2).to_broadcast([P, TOPK, EXPERTS]), ALU.is_equal), until=False)
                if known == 0:
                    dve.wait_ge(s["masked"], 5 + 2 * CHUNKS)
                    values(0)
                if live(known, 0):
                    dve.wait_ge(s["pv_ps"], i + 1)
                    o_heads = v3(o_b[:, 0:HEADS * HV], HEADS)
                    dve.reciprocal(row_inv[:, :].unsqueeze(2), o_heads[:, :, HD:HV]).then_inc(s["inv_done"], 1)
                if live(known, -2):
                    dve.wait_ge(s["route_step"], (i - 2) * ROUTE_LINKS + 6)
                    link(tt(v3(picked[:, :], TOPK), v3(hot, TOPK),
                            score[:, :].unsqueeze(1).to_broadcast([P, TOPK, EXPERTS]), ALU.mult), until=False)
                if live(known, 0):
                    dve.wait_ge(s["inv_done"], i + 1)
                    tt(v3(attn[:, :], HEADS), o_heads[:, :, 0:HD],
                       row_inv[:, :].unsqueeze(2).to_broadcast([P, HEADS, HD]), ALU.mult).then_inc(s["normed"], 1)
                if live(known, -2):
                    dve.wait_ge(s["route_step"], (i - 2) * ROUTE_LINKS + 7)
                    link(dve.tensor_reduce(scores2[:, cols(i - 2, TOPK)], v3(picked[:, :], TOPK),
                                           axis=AXX, op=ALU.add), until=False)
                    need(dve, s["rank_ps"], i - 2)
                    link(tt(mask_sum[:, :], mask_sum[:, :], mask_bf[:, :], ALU.add), until=False)
                if live(known, -2):
                    dve.wait_ge(s["y_ps"], i - 1)
                    x2 = resid[:, cols(i - 2)]
                    tt(x2, x2, h_b[:, 0:DIM], ALU.add).then_inc(s["acc_done"], 1)
                    dve.wait_ge(s["route_step"], (i - 2) * ROUTE_LINKS + 9)
                    link(tt(mask_bf[:, :], hot0, hot1, ALU.add), until=False)
                if known == FIRST:
                    dve.wait_ge(s["k_out"], 2)
                    tt(k_raw_lo[:, :], k_raw[:, :], k_raw_hi[:, :].bitcast(F32), ALU.subtract).then_inc(s["k_low"], 1)
                    dve.wait_ge(s["masked"], 4)
                    dve.wait_ge(s["k_low"], 1)

                    keys(0)
                    dve.wait_ge(s["gate_high"], 1)
                    tt(gate_lo[:, :], gate_raw[:, :], gate_hi[:, :].bitcast(F32), ALU.subtract).then_inc(s["gate_low"], 1)
                    dve.wait_ge(s["bias_in"], 16)
                    dve.wait_ge(s["filled"], 14)
                if known == 0:
                    keys(1)
                    values(1)

            run_phase_a(dve, step)

            def ranks_read(t, source):
                dve.wait_ge(s["rank_ps"], t + 1)
                tt(v3(picked_r[:, :], TOPK), v3(onehot[:, cols(t % 2, TOPK * EXPERTS)], TOPK),
                   source[:, 0:EXPERTS].unsqueeze(1).to_broadcast([P, TOPK, EXPERTS]),
                   ALU.mult).then_inc(s["rank_read"], 1)
                dve.wait_ge(s["rank_read"], t + 1)

            def places(t):
                place = chain(s["dest_step"], t * 3)
                place(dve.tensor_reduce(ranks2[:, :], v3(picked_r[:, :], TOPK), axis=AXX, op=ALU.add))
                place(stt(dest_f[:, :], chosen_f[:, :], float(REGION), ranks2[:, :], ALU.mult, ALU.add))
                dve.wait_ge(scat[t % 2], 16 * TOPK * (t // 2))
                place(dve.tensor_copy(dest[:, cols(t % 2, TOPK)], dest_f[:, :]), until=False)

            def low_part(to, source, high, ready, value, done):
                dve.wait_ge(s[ready], value)
                tt(to, source, high.bitcast(F32), ALU.subtract).then_inc(s[done], 1)

            def scores_of(t, link):
                dve.wait_ge(s["tanh_g"], t + 1)
                link(ts(score[:, :], th8[:, :], 0.5, 0.5, ALU.mult, ALU.add))
                link(tt(ranked[:, :], score[:, :], bias_b[:, :], ALU.add))

            def experts_of(t, link):
                hot = onehot[:, cols(t % 2, TOPK * EXPERTS)]
                link(dve.max(top8[:, :], ranked[:, :]))
                link(dve.max_index(top8_i[:, :], top8[:, :], ranked[:, :]))
                link(dve.tensor_copy(chosen_f[:, :], top8_i[:, 0:TOPK]))
                link(tt(v3(hot, TOPK), iota_e[:, :].unsqueeze(1).to_broadcast([P, TOPK, EXPERTS]),
                        chosen_f[:, :].unsqueeze(2).to_broadcast([P, TOPK, EXPERTS]), ALU.is_equal))

            def picks_of(t, link):
                link(tt(v3(picked[:, :], TOPK), v3(onehot[:, cols(t % 2, TOPK * EXPERTS)], TOPK),
                        score[:, :].unsqueeze(1).to_broadcast([P, TOPK, EXPERTS]), ALU.mult))
                link(dve.tensor_reduce(scores2[:, cols(t, TOPK)], v3(picked[:, :], TOPK), axis=AXX, op=ALU.add),
                     until=False)

            def mask_of(t, link):
                hot = onehot[:, cols(t % 2, TOPK * EXPERTS)]
                dve.wait_ge(s["rank_ps"], t)
                link(tt(mask_sum[:, :], mask_sum[:, :], mask_bf[:, :], ALU.add))
                link(tt(mask_bf[:, :], hot[:, 0:EXPERTS], hot[:, EXPERTS:], ALU.add), until=False)

            def gated(t, source):
                dve.wait_ge(s["tanh_h"], t + 1)
                stt(silu_s[:, :], act_s[:, :], 1.0, source[:, 0:DIM], ALU.add, ALU.mult).then_inc(s["silu_done"], 1)
                dve.wait_ge(s["silu_done"], t + 1)
                stt(hid[:, cols(t % 2)], silu_s[:, :], 0.5, source[:, DIM:2 * DIM],
                    ALU.mult, ALU.mult).then_inc(s["hid_done"], 1)

            def shared_added(t, source):
                dve.wait_ge(s["y_ps"], t + 1)
                acc = resid[:, cols(t)]
                tt(acc, acc, source[:, 0:DIM], ALU.add).then_inc(s["acc_done"], 1)

            ranks_read(TILE_A - 1, t_b)
            low_part(x2_lo[:, cols(0)], t_b[:, 0:DIM], x2_hi[:, cols(0)], "x2_high", TILES - 1, "x2_low")
            places(TILE_A - 1)
            x1 = resid[:, cols(TILE_B)]
            norm = chain(s["ln2_step"], TILE_B * 3)
            dve.wait_ge(s["o_ps"], TILES)
            tt(x1, x1, o_b[:, 0:DIM], ALU.add).then_inc(s["x1_done"], 1)
            dve.wait_ge(s["x1_done"], TILES)
            norm(dve.bn_stats(stats2[:, :], x1))
            norm(dve.bn_aggr(mv2[:, :], stats2[:, :]))
            norm(ts(ve2[:, :], mv2[:, 1:2], EPS, None, ALU.add), until=False)
            link_a = chain(s["route_step"], TILE_A * ROUTE_LINKS)
            scores_of(TILE_A, link_a)
            dve.wait_ge(s["pow2"], TILES)
            dve.wait_ge(s["scaled_done"], 3 * TOPK * TILE_A)
            ts(xn2[:, (TILE_B % 2) * (DIM + 1):(TILE_B % 2) * (DIM + 1) + DIM], x1, mv2[:, 0:1], rstd2[:, :],
               ALU.subtract, ALU.mult).then_inc(s["xn2_done"], 1)
            experts_of(TILE_A, link_a)
            picks_of(TILE_A, link_a)
            mask_of(TILE_A, link_a)
            low_part(x2_lo[:, cols(1)], q_b[:, 0:DIM], x2_hi[:, cols(1)], "x2_high", TILES, "x2_low")
            ranks_read(TILE_A, bank[1])
            places(TILE_A)
            link_b = chain(s["route_step"], TILE_B * ROUTE_LINKS)
            gated(TILE_A, h_b)
            scores_of(TILE_B, link_b)
            experts_of(TILE_B, link_b)
            mask_of(TILE_B, link_b)
            picks_of(TILE_B, link_b)
            ranks_read(TILE_B, bank[2])
            places(TILE_B)
            low_part(h_lo[:, :], t_b[:, 0:DIM], h_hi[:, :], "h_high", TILES - 1, "h_low")
            gated(TILE_B, bank[0])
            shared_added(TILE_A, h_b)

            link = chain(s["table_step"], 0)
            link(dve.tensor_copy(counts[:, :], bank[2][:, EXPERTS:2 * EXPERTS]))
            link(tt(v3(over[:, :], EXPERTS), counts[:, :].unsqueeze(2).to_broadcast([P, EXPERTS, TILES]),
                    iota_m[:, :].unsqueeze(1).to_broadcast([P, EXPERTS, TILES]), ALU.is_gt))
            link(dve.tensor_reduce(n_tiles[:, :], v3(over[:, :], EXPERTS), axis=AXX, op=ALU.add))
            low_part(h_lo[:, :], q_b[:, 0:DIM], h_hi[:, :], "h_high", TILES, "h_low")
            link(dve.tensor_tensor_scan(end_tile[:, :], ones_e[:, :], n_tiles[:, :], 0.0, ALU.mult, ALU.add))
            link(tt(v3(passed[:, :], TILES_B), iota_j[:, :].unsqueeze(2).to_broadcast([P, TILES_B, EXPERTS]),
                    end_tile[:, :].unsqueeze(1).to_broadcast([P, TILES_B, EXPERTS]), ALU.is_ge))
            link(dve.tensor_reduce(expert_f[:, :], v3(passed[:, :], TILES_B), axis=AXX, op=ALU.add), until=False)
            link(tt(v3(passed_n[:, :], TILES_B), v3(passed[:, :], TILES_B),
                    n_tiles[:, :].unsqueeze(1).to_broadcast([P, TILES_B, EXPERTS]), ALU.mult))
            link(dve.tensor_reduce(before_f[:, :], v3(passed_n[:, :], TILES_B), axis=AXX, op=ALU.add))
            link(tt(row_f[:, :], iota_j[:, :], before_f[:, :], ALU.subtract))
            link(ts(before_f[:, :], expert_f[:, :], float(REGION), None, ALU.mult))
            link(stt(row_f[:, :], row_f[:, :], float(P), before_f[:, :], ALU.mult, ALU.add))
            link(ts(row_i[:, :], row_f[:, :], float(EXPERTS * REGION), None, ALU.min), until=False)
            link(ts(column_i[:, :], expert_f[:, :], float(EXPERTS - 1), float(EW), ALU.min, ALU.mult), until=False)
            shared_added(TILE_B, bank[0])

            def x_low(j, par):
                dve.wait_ge(s["b_x_high"], j + 1)
                tt(x2_lo[:, cols(par)], q_b[:, 0:DIM], x2_hi[:, cols(par)].bitcast(F32),
                   ALU.subtract).then_inc(s["b_x_low"], 1)

            def keep_meta(j, buf):
                dve.wait_ge(s["b_t_ps"], j + 1)
                a = buf * ROW + (ID_EVEN, SCORE)[buf % 2]
                dve.tensor_copy(meta[:, cols(j, 2)].bitcast(I32),
                                list_rows[:, a:a + 2].bitcast(I32)).then_inc(s["b_meta"], 1)

            def hidden(j, par):
                dve.wait_ge(s["b_silu"], j + 1)
                need(dve, s["b_ht_ps"], j - 1)
                tt(hid[:, cols(par)], act_s[:, :], hidden_b[par][:, DIM:2 * DIM], ALU.mult).then_inc(s["b_hid"], 1)

            def step_b(j, buf, known):
                par = buf % 2
                dve.wait_ge(s["b_h_high"], j + 1)
                tt(h_lo[:, :], t_b[:, 0:DIM], h_hi[:, :].bitcast(F32), ALU.subtract).then_inc(s["b_h_low"], 1)
                if known is None or known + 3 < TILES_B:
                    x_low(j + 3, 1 - par)
                    keep_meta(j + 3, (buf + 3) % LIST_BUFS)
                if known is None or known + 2 < TILES_B:
                    hidden(j + 2, par)

            for j in range(3):
                x_low(j, j % 2)
                keep_meta(j, j)
                if j < 2:
                    hidden(j, j)

            run_phase_b(dve, step_b)

            for n, (t, tiles) in enumerate(SUM_GROUPS):
                acc, rows = v3(resid[:, :], TILES)[:, t:t + tiles, :], sum_tiles[:, t:t + tiles, :]
                dve.wait_ge(c_in[n], 16)
                tt(acc, acc, rows[:, :, 0:DIM], ALU.add).then_inc(s["c_first"], 1)
                dve.wait_ge(s["c_first"], n + 1)
                tt(acc, acc, rows[:, :, DIM:], ALU.add).then_inc(s["c_sum"], 1)

        @block.tensor
        def _(pe):
            mm = pe.matmul

            def product(to, stationary, moving, start=True, stop=True):
                (ah, al), (bh, bl) = stationary, moving
                mm(to, ah, bl, start=start, stop=False)
                mm(to, al, bh, start=False, stop=False)
                return mm(to, ah, bh, start=False, stop=stop)

            def transposed(to, rows):
                for kt in range(KT):
                    last = pe.transpose(to[:, cols(kt, P)], rows[:, cols(kt, P)], ident[:, :])
                return last

            pe.wait_ge(s["ctx_in"], 16)
            pe.wait_ge(s["wk_in"], 16)
            for half in range(2):
                for kt in range(KT):
                    last = mm(h_b[:, cols(half, BATCH * KEYS)],
                              wk[:, kt * DIM + half * P:kt * DIM + (half + 1) * P],
                              ctx_t[:, cols(kt, BATCH * KEYS)], start=kt == 0, stop=kt == KT - 1)
            last.then_inc(s["k_ps"], 1)

            def values():
                pe.wait_ge(s["wv_in"], 16)
                for b in range(BATCH):
                    for kt in range(KT):
                        last = mm(bank[0][0:KEYS, cols(b)], ctx_t[:, cols(kt * BATCH + b, KEYS)],
                                  wv[:, cols(kt)], start=kt == 0, stop=kt == KT - 1)
                last.then_inc(s["v_ps"], 1)

            def scores(half, batch):
                for r in range(2):
                    rows = slice(64 * r, 64 * r + 64)
                    q = [t[rows, cols(half, P)] for t in (q_hi, q_lo)]
                    k = [t[rows, cols(batch * 2 + half, BANK_COLS)] for t in (k_hi, k_lo)]
                    last = product(bank[2 * half + r][:, 0:BANK_COLS], q, k)
                return last

            def projected():
                for kt in range(KT):
                    last = mm(o_b[:, 0:DIM], attn_t[:, cols(kt, P)], wo[:, cols(kt)],
                              start=kt == 0, stop=kt == KT - 1)
                last.then_inc(s["o_ps"], 1)

            def shared_gate_up(to, buf):
                for kt in range(KT):
                    w = EXPERTS * EW + kt * UP
                    last = product(to, [t[:, cols(buf * KT + kt, P)] for t in (x2_hi, x2_lo)],
                                   [t[:, w:w + UP] for t in (w_hi, w_lo)],
                                   start=kt == 0, stop=kt == KT - 1)
                return last

            def shared_down(to):
                for kt in range(KT):
                    w = EXPERTS * EW + KT * UP + kt * DIM
                    last = product(to[:, 0:DIM], [t[:, cols(kt, P)] for t in (h_hi, h_lo)],
                                   [t[:, w:w + DIM] for t in (w_hi, w_lo)],
                                   start=kt == 0, stop=kt == KT - 1)
                return last

            def router(buf):
                for kt in range(KT):
                    last = product(t_b[:, 0:EXPERTS], [t[:, cols(buf * KT + kt, P)] for t in (x2_hi, x2_lo)],
                                   [t[:, cols(kt, EXPERTS)] for t in (gate_hi, gate_lo)],
                                   start=kt == 0, stop=kt == KT - 1)
                return last

            def ranks(to):
                mm(to, upper[:, :], mask_bf[:, :], start=True, stop=False)
                return mm(to, ones[:, :], mask_sum[:, :], start=False, stop=True)

            def counts(to):
                mm(to[:, EXPERTS:2 * EXPERTS], ones[:, :], mask_sum[:, :], start=True, stop=False)
                mm(to[:, EXPERTS:2 * EXPERTS], ones[:, :], mask_bf[:, :], start=False, stop=True)

            def step(i, par, known, batch):
                if live(known, 0):
                    if known == 0:
                        pe.wait_ge(s["k_masked"], 4)
                        pe.wait_ge(s["v_out"], 1)
                    if known is None and batch == 1:
                        pe.wait_ge(s["k_masked"], 8)
                    pe.wait_ge(s["q_low"], i + 1)
                    need(pe, s["pt_out"], 3 * i)
                    scores(0, batch)
                if live(known, -1):
                    pe.wait_ge(s["normed"], i)
                    transposed(q_b, attn).then_inc(s["ot_ps"], 1)
                if live(known, -3):
                    pe.wait_ge(s["route_step"], (i - 2) * ROUTE_LINKS)
                    if known == LAST - 1:
                        counts(t_b)
                    ranks(t_b[:, 0:EXPERTS]).then_inc(s["rank_ps"], 1)
                if live(known, 0):
                    scores(1, batch).then_inc(s["s_ps"], 1)
                if live(known, 1):
                    if known == -1:
                        pe.wait_ge(s["masked"], 1)
                    pe.wait_ge(s["xn1"], i + 2)
                    need(pe, s["ot_out"], i)
                    transposed(q_b, xn).then_inc(s["t1_ps"], 1)
                if live(known, -2):
                    pe.wait_ge(s["xn2_done"], i - 1)
                    need(pe, s["rank_read"], i - 2)
                    transposed(t_b, xn2[:, cols(par, DIM + 1)]).then_inc(s["t2_ps"], 1)
                if live(known, -1):
                    if known == 1:
                        pe.wait_ge(s["wo_in"], 16)
                    pe.wait_ge(s["ot_out"], i)
                    projected()
                if live(known, 1):
                    if known == -1:
                        pe.wait_ge(s["wq_in"], 16)
                    pe.wait_ge(s["t1_out"], i + 2)
                    for half in range(2):
                        for kt in range(KT):
                            last = mm(q_b[:, cols(half, P)], wq[:, kt * DIM + half * P:kt * DIM + (half + 1) * P],
                                      xn_t[:, cols(kt, P)], start=kt == 0, stop=kt == KT - 1)
                    last.then_inc(s["q_ps"], 1)
                if live(known, -2):
                    if known == 2:
                        pe.wait_ge(s["shared_lo"], 1)
                        pe.wait_ge(s["gate_low"], 1)
                    pe.wait_ge(s["x2_low"], i - 1)
                    need(pe, s["acc_done"], i - 2)
                    shared_gate_up(h_b, 0).then_inc(s["h_ps"], 1)
                    router(0).then_inc(s["gate_ps"], 1)
                if live(known, 0):
                    if known == 0:
                        pe.wait_ge(s["filled"], 14)
                    for c in range(CHUNKS):
                        if c in (0, 4):
                            pe.wait_ge(s["exped"], 2 * i + 1 + c // 4)
                        last = pe.transpose(bank[c // 4][:, cols(c % 4, P)], probs[:, cols(c, P)], ident[:, :])
                        if c % 4 == 3 or c == CHUNKS - 1:
                            last.then_inc(s["pt_ps"], 1)
                if live(known, -2):
                    pe.wait_ge(s["hid_done"], i - 1)
                    pe.wait_ge(s["tanh_g"], i - 1)
                    transposed(t_b, hid).then_inc(s["ht_ps"], 1)
                if live(known, 0):
                    if known == 0:
                        pe.wait_ge(s["v_done"], VHEADS + 1)
                    if known is None and batch == 1:
                        pe.wait_ge(s["v_done"], 2 * (VHEADS + 1))
                    need(pe, s["x1_done"], i)
                    for c in range(CHUNKS):
                        if c % 4 == 0:
                            pe.wait_ge(s["pt_out"], 3 * i + c // 4 + 1)
                        last = mm(o_b[:, head_base(c) * HV:(head_base(c) + VHEADS) * HV],
                                  probs_t[:, cols(c, P)], vals[:, cols(batch * CHUNKS + c, VHEADS * HV)],
                                  start=c == 0, stop=c == CHUNKS - 1, skip_group_check=True)
                    last.then_inc(s["pv_ps"], 1)
                if live(known, -2):
                    pe.wait_ge(s["h_low"], i - 1)
                    shared_down(h_b).then_inc(s["y_ps"], 1)

            values()
            run_phase_a(pe, step)

            pe.wait_ge(s["route_step"], TILE_A * ROUTE_LINKS)
            ranks(t_b[:, 0:EXPERTS]).then_inc(s["rank_ps"], 1)
            pe.wait_ge(s["normed"], TILES)
            transposed(q_b, attn).then_inc(s["ot_ps"], 1)
            pe.wait_ge(s["xn2_done"], TILES - 1)
            pe.wait_ge(s["rank_read"], TILE_A)
            transposed(t_b, xn2[:, cols(TILE_A % 2, DIM + 1)]).then_inc(s["t2_ps"], 1)
            pe.wait_ge(s["ot_out"], TILES)
            projected()
            pe.wait_ge(s["x2_low"], TILES - 1)
            router(0).then_inc(s["gate_ps"], 1)
            pe.wait_ge(s["acc_done"], TILE_A)
            shared_gate_up(h_b, 0).then_inc(s["h_ps"], 1)
            pe.wait_ge(s["xn2_done"], TILES)
            transposed(q_b, xn2[:, cols(TILE_B % 2, DIM + 1)]).then_inc(s["t2_ps"], 1)
            pe.wait_ge(s["route_step"], TILE_B * ROUTE_LINKS)
            ranks(bank[1][:, 0:EXPERTS]).then_inc(s["rank_ps"], 1)
            pe.wait_ge(s["x2_low"], TILES)
            pe.wait_ge(s["tanh_g"], TILES - 1)
            router(1).then_inc(s["gate_ps"], 1)
            shared_gate_up(bank[0], 1).then_inc(s["h_ps"], 1)
            pe.wait_ge(s["route_step"], TILE_B * ROUTE_LINKS + LAST_ROUTE_MASK)
            counts(bank[2])
            ranks(bank[2][:, 0:EXPERTS]).then_inc(s["rank_ps"], 1)
            for t, rows_b, to in ((TILE_A, t_b, h_b), (TILE_B, q_b, bank[0])):
                pe.wait_ge(s["hid_done"], t + 1)
                pe.wait_ge(s["tanh_g"], TILES)
                transposed(rows_b, hid[:, cols(t % 2)]).then_inc(s["ht_ps"], 1)
                pe.wait_ge(s["h_low"], t + 1)
                shared_down(to).then_inc(s["y_ps"], 1)
            for _ in range(BUSY_PRODUCTS):
                mm(bank[3][:, 0:P], ones[:, :], ones[:, :])
            pe.wait_ge(s["split_lo"], SPLIT_STEPS)
            pe.wait_ge(s["table_step"], TABLE_TILES)

            def rows_transposed(j):
                need(pe, s["b_x_low"], j)
                pe.wait_ge(b_in[j % LIST_BUFS], 16 * (j // LIST_BUFS + 1))
                transposed(q_b, list_rows[:, cols(j % LIST_BUFS, ROW)]).then_inc(s["b_t_ps"], 1)

            def first_column(j):
                return pe.value_load(column_i[0:1, j:j + 1], min_val=0, max_val=(EXPERTS - 1) * EW)

            def gate_up(j, column):
                par = j % 2
                for kt in range(KT):
                    last = product(hidden_b[par], [t[:, cols(par * KT + kt, P)] for t in (x2_hi, x2_lo)],
                                   [t[:, bass.ds(column + kt * UP, UP)] for t in (w_hi, w_lo)],
                                   start=kt == 0, stop=kt == KT - 1)
                last.then_inc(s["b_h_ps"], 1)

            rows_transposed(0)
            for j in range(2):
                rows_transposed(j + 1)
                gate_up(j, first_column(j))
            column_ahead = first_column(2)
            for j in range(TILES_B):
                pe.wait_ge(s["b_hid"], j + 1)
                transposed(t_b, hid[:, cols(j % 2)]).then_inc(s["b_ht_ps"], 1)
                if j + 3 < TILES_B:
                    rows_transposed(j + 3)
                if j + 2 < TILES_B:
                    if j + 3 == TILES_B:
                        pe.wait_ge(s["b_x_low"], TILES_B)
                    gate_up(j + 2, column_ahead)
                column = first_column(j)
                if j + 3 < TILES_B:
                    column_ahead = first_column(j + 3)
                pe.wait_ge(s["b_h_low"], j + 1)
                for kt in range(KT):
                    last = product(o_b[:, 0:DIM], [t[:, cols(kt, P)] for t in (h_hi, h_lo)],
                                   [t[:, bass.ds(column + KT * UP + kt * DIM, DIM)] for t in (w_hi, w_lo)],
                                   start=kt == 0, stop=kt == KT - 1)
                last.then_inc(s["b_y_ps"], 1)


_OUT = ((BATCH, SEQ, DIM), "float32")


def _partition_first(w_t):
    n = w_t.shape[-1]
    return np.ascontiguousarray(w_t.reshape(KT, P, n).transpose(1, 0, 2).reshape(P, KT * n))


def kernel(**inputs):
    import concourse.bacc as bacc
    from concourse.bass_utils import run_bass_kernel_spmd

    a = {k.removeprefix("L0_"): np.asarray(v) for k, v in inputs.items()}
    x = np.ascontiguousarray(a["x"].reshape(TOKENS, DIM))
    ctx = a["ctx_1024"].transpose(2, 0, 1).reshape(DIM, BATCH * KEYS)

    def expert(w1, w3, w2):
        up = _partition_first(np.concatenate([w1.T, w3.T], axis=1))
        return np.concatenate([up, _partition_first(w2.T)], axis=1)

    experts = [expert(a["ffn_w1"][e], a["ffn_w3"][e], a["ffn_w2"][e]) for e in range(EXPERTS)]
    shared = expert(a["ffn_sw1"], a["ffn_sw3"], a["ffn_sw2"])
    arrays = {
        "in_x": x,
        "in_ctx": _partition_first(ctx),
        "in_wq": _partition_first(a["xattn_w_q"].T),
        "in_wk": _partition_first(a["xattn_w_k"].T),
        "in_wv": _partition_first(a["xattn_w_v"].T),
        "in_wo": _partition_first(a["xattn_w_o"].T),
        "in_gate": _partition_first(a["ffn_gate_w"].T),
        "in_bias": np.ascontiguousarray(a["ffn_expert_bias"]),
        "in_ffn": np.ascontiguousarray(np.concatenate(experts + [shared], axis=1)),
    }
    nc = bacc.Bacc("TRN2", target_bir_lowering=False, num_devices=1)
    args = [nc.dram_tensor(n, v.shape, mybir.dt.from_np(v.dtype), kind="ExternalInput").ap()
            for n, v in arrays.items()]
    out = nc.dram_tensor("out_x", (TOKENS, DIM), mybir.dt.from_np(np.dtype(_OUT[1])), kind="ExternalOutput").ap()
    layer_kernel(nc, *args, out)
    r = run_bass_kernel_spmd(nc, [arrays], core_ids=[0])
    return r.results[0]["out_x"].reshape(_OUT[0])
```
